# Optimizing a Trainium2 kernel written in Bass

```python
import numpy as np
import jax
import jax.numpy as jnp

def _softmax(x, axis=-1):
    return jax.nn.softmax(x, axis=axis)

def _gelu(x):
    return jax.nn.gelu(x, approximate=True)

def _silu(x):
    return jax.nn.silu(x)

def _sigmoid(x):
    return jax.nn.sigmoid(x)

def _layernorm(x, axis=-1, eps=1e-05):
    m = jnp.mean(x, axis=axis, keepdims=True)
    v = jnp.var(x, axis=axis, keepdims=True)
    return (x - m) / jnp.sqrt(v + eps)

def _scatter_add(tgt, idx, src, axis=0):
    return tgt.at[idx].add(src)

def _segment_sum(src, seg, n):
    return jax.ops.segment_sum(src, seg, n)
kernel_name = 'mk_hybrid_d1_jaxref_r8_a69146'

def setup_inputs(seed: int=0):
    np.random.seed(seed)
    _w = jnp.asarray

    def _L0_attn_a_setup():
        import jax, jax.numpy as jnp
        import numpy as np
        H = 4

        def rmsnorm(x, scale, eps=1e-08):
            norm = jnp.linalg.norm(x, axis=-1, keepdims=True) / jnp.sqrt(jnp.float32(x.shape[-1]))
            return scale * (x / (norm + eps))

        def wkv_scan(q, k, v, w):
            B, T, _, D = q.shape
            qT = jnp.swapaxes(q, 0, 1)
            kT = jnp.swapaxes(k, 0, 1)
            vT = jnp.swapaxes(v, 0, 1)

            def step(carry, inp):
                A, z = carry
                qt, kt, vt = inp
                A = w[None, :, :, None] * A + kt[..., None] * vt[..., None, :]
                z = w[None] * z + kt
                S = jnp.einsum('bhd,bhde->bhe', qt, A)
                return ((A, z), (S, z))
            A0 = jnp.zeros((B, H, D, D), q.dtype)
            z0 = jnp.zeros((B, H, D), q.dtype)
            _, (S, Z) = jax.lax.scan(step, (A0, z0), (qT, kT, vT))
            return (jnp.swapaxes(S, 0, 1), jnp.swapaxes(Z, 0, 1))
        key = jax.random.key(seed)
        ks = jax.random.split(key, 12)
        B, T, C = (4, 256, 128)
        inv_sqrt_c = 1.0 / np.sqrt(C)
        return {'x': jax.random.normal(ks[0], (B, T, C), jnp.float32), 'time_decay': jax.random.normal(ks[1], (C,), jnp.float32) * 0.5, 'mix_q': jax.random.uniform(ks[2], (1, 1, C), jnp.float32), 'mix_k': jax.random.uniform(ks[3], (1, 1, C), jnp.float32), 'mix_v': jax.random.uniform(ks[4], (1, 1, C), jnp.float32), 'mix_g': jax.random.uniform(ks[5], (1, 1, C), jnp.float32), 'Wq': jax.random.normal(ks[6], (C, C), jnp.float32) * inv_sqrt_c, 'Wk': jax.random.normal(ks[7], (C, C), jnp.float32) * inv_sqrt_c, 'Wv': jax.random.normal(ks[8], (C, C), jnp.float32) * inv_sqrt_c, 'Wg': jax.random.normal(ks[9], (C, C), jnp.float32) * inv_sqrt_c, 'Wo': jax.random.normal(ks[10], (C, C), jnp.float32) * inv_sqrt_c, 'norm_scale': jnp.ones((C,), jnp.float32)}
    _L0_attn_a_in = _L0_attn_a_setup()

    def _L0_attn_b_setup():
        import jax, jax.numpy as jnp
        import numpy as np
        FEATURE_DIM = 16
        NUM_HEADS = 16
        HEAD_DIM = 64
        R2 = float(np.sqrt(2.0))
        RD = float(np.sqrt(FEATURE_DIM))
        RRD = float(np.sqrt(RD))
        RMS_EPS = 1e-05

        def taylor_exp(x):
            x2 = (x[..., :, None] * x[..., None, :]).reshape(*x.shape[:-1], FEATURE_DIM * FEATURE_DIM) / R2
            ones = jnp.ones_like(x[..., :1])
            return jnp.concatenate([ones, x / RRD, x2 / RD], axis=-1)

        def _reference_tuple_inner(hidden_states, Wq, Wk, Wv, Wo, g_weight):
            b, l, _ = hidden_states.shape
            q = (hidden_states @ Wq.T).reshape(b, l, NUM_HEADS, FEATURE_DIM).transpose(0, 2, 1, 3)
            k = (hidden_states @ Wk.T).reshape(b, l, NUM_HEADS, FEATURE_DIM).transpose(0, 2, 1, 3)
            v = (hidden_states @ Wv.T).reshape(b, l, NUM_HEADS, HEAD_DIM).transpose(0, 2, 1, 3)
            qf = taylor_exp(q)
            kf = taylor_exp(k)
            A_qk = jnp.einsum('bhnd,bhmd->bhnm', qf, kf)
            A_qk = jnp.tril(A_qk)
            y = jnp.einsum('bhnm,bhme->bhne', A_qk, v)
            kv_state = jnp.einsum('bhnd,bhnf->bhfd', kf, v)[:, :, None]
            rms = jax.lax.rsqrt(jnp.mean(y * y, axis=-1, keepdims=True) + RMS_EPS)
            y = y * rms * g_weight
            y = y.transpose(0, 2, 1, 3).reshape(b, l, NUM_HEADS * HEAD_DIM)
            out = y @ Wo.T
            return (out, kv_state)
        key = jax.random.key(seed)
        ks = jax.random.split(key, 5)
        b, l, d_model = (4, 256, 128)
        inp = {'hidden_states': jax.random.normal(ks[0], (b, l, d_model), dtype=jnp.float32), 'Wq': jax.random.normal(ks[1], (FEATURE_DIM * NUM_HEADS, d_model), dtype=jnp.float32) * 0.02, 'Wk': jax.random.normal(ks[2], (FEATURE_DIM * NUM_HEADS, d_model), dtype=jnp.float32) * 0.02, 'Wv': jax.random.normal(ks[3], (NUM_HEADS * HEAD_DIM, d_model), dtype=jnp.float32) * 0.02, 'Wo': jax.random.normal(ks[4], (d_model, NUM_HEADS * HEAD_DIM), dtype=jnp.float32) * 0.02, 'g_weight': jnp.ones((HEAD_DIM,), dtype=jnp.float32)}
        return inp
    _L0_attn_b_in = _L0_attn_b_setup()

    def _L0_ffn_setup():
        import jax, jax.numpy as jnp
        import numpy as np
        B, S, D, H, O, E, K = (4, 256, 128, 256, 128, 8, 2)
        key = jax.random.key(seed)
        ks = jax.random.split(key, 8)
        x = jax.random.normal(ks[0], (B, S, D), dtype=jnp.float32)
        gate_w = jax.random.uniform(ks[1], (E, D), dtype=jnp.float32, minval=-1, maxval=1) * np.sqrt(6.0 / D)
        gate_b = jnp.zeros((E,), dtype=jnp.float32)
        w1 = jax.random.uniform(ks[2], (E, D, H), dtype=jnp.float32, minval=-1, maxval=1) * np.sqrt(6.0 / D)
        b1 = jnp.zeros((E, H), dtype=jnp.float32)
        w2 = jax.random.uniform(ks[3], (E, H, O), dtype=jnp.float32, minval=-1, maxval=1) * np.sqrt(6.0 / H)
        b2 = jnp.zeros((E, O), dtype=jnp.float32)
        return {'x': x, 'gate_w': gate_w, 'gate_b': gate_b, 'w1': w1, 'b1': b1, 'w2': w2, 'b2': b2}
    _L0_ffn_in = _L0_ffn_setup()
    _d = {'L0_attn_a_x': _L0_attn_a_in['x'], 'L0_attn_a_time_decay': _L0_attn_a_in['time_decay'], 'L0_attn_a_mix_q': _L0_attn_a_in['mix_q'], 'L0_attn_a_mix_k': _L0_attn_a_in['mix_k'], 'L0_attn_a_mix_v': _L0_attn_a_in['mix_v'], 'L0_attn_a_mix_g': _L0_attn_a_in['mix_g'], 'L0_attn_a_Wq': _L0_attn_a_in['Wq'], 'L0_attn_a_Wk': _L0_attn_a_in['Wk'], 'L0_attn_a_Wv': _L0_attn_a_in['Wv'], 'L0_attn_a_Wg': _L0_attn_a_in['Wg'], 'L0_attn_a_Wo': _L0_attn_a_in['Wo'], 'L0_attn_a_norm_scale': _L0_attn_a_in['norm_scale'], 'L0_attn_b_Wq': _L0_attn_b_in['Wq'], 'L0_attn_b_Wk': _L0_attn_b_in['Wk'], 'L0_attn_b_Wv': _L0_attn_b_in['Wv'], 'L0_attn_b_Wo': _L0_attn_b_in['Wo'], 'L0_attn_b_g_weight': _L0_attn_b_in['g_weight'], 'L0_ffn_gate_w': _L0_ffn_in['gate_w'], 'L0_ffn_gate_b': _L0_ffn_in['gate_b'], 'L0_ffn_w1': _L0_ffn_in['w1'], 'L0_ffn_b1': _L0_ffn_in['b1'], 'L0_ffn_w2': _L0_ffn_in['w2'], 'L0_ffn_b2': _L0_ffn_in['b2']}
    _x0 = _d['L0_attn_a_x']
    _d['L0_attn_a_x'] = jax.random.normal(jax.random.fold_in(jax.random.key(seed), 1), (4, 512, 128), dtype=_x0.dtype)
    del _x0
    return _d

def reference(L0_attn_a_x, L0_attn_a_time_decay, L0_attn_a_mix_q, L0_attn_a_mix_k, L0_attn_a_mix_v, L0_attn_a_mix_g, L0_attn_a_Wq, L0_attn_a_Wk, L0_attn_a_Wv, L0_attn_a_Wg, L0_attn_a_Wo, L0_attn_a_norm_scale, L0_attn_b_Wq, L0_attn_b_Wk, L0_attn_b_Wv, L0_attn_b_Wo, L0_attn_b_g_weight, L0_ffn_gate_w, L0_ffn_gate_b, L0_ffn_w1, L0_ffn_b1, L0_ffn_w2, L0_ffn_b2):

    def _L0_attn_a_ref(x, time_decay, mix_q, mix_k, mix_v, mix_g, Wq, Wk, Wv, Wg, Wo, norm_scale):
        import jax, jax.numpy as jnp
        import numpy as np
        H = 4

        def rmsnorm(x, scale, eps=1e-08):
            norm = jnp.linalg.norm(x, axis=-1, keepdims=True) / jnp.sqrt(jnp.float32(x.shape[-1]))
            return scale * (x / (norm + eps))

        def wkv_scan(q, k, v, w):
            B, T, _, D = q.shape
            qT = jnp.swapaxes(q, 0, 1)
            kT = jnp.swapaxes(k, 0, 1)
            vT = jnp.swapaxes(v, 0, 1)

            def step(carry, inp):
                A, z = carry
                qt, kt, vt = inp
                A = w[None, :, :, None] * A + kt[..., None] * vt[..., None, :]
                z = w[None] * z + kt
                S = jnp.einsum('bhd,bhde->bhe', qt, A)
                return ((A, z), (S, z))
            A0 = jnp.zeros((B, H, D, D), q.dtype)
            z0 = jnp.zeros((B, H, D), q.dtype)
            _, (S, Z) = jax.lax.scan(step, (A0, z0), (qT, kT, vT))
            return (jnp.swapaxes(S, 0, 1), jnp.swapaxes(Z, 0, 1))
        B, T, C = x.shape
        D = C // H
        xx = jnp.pad(x, ((0, 0), (1, 0), (0, 0)))[:, :-1]
        xq = x * mix_q + xx * (1.0 - mix_q)
        xk = x * mix_k + xx * (1.0 - mix_k)
        xv = x * mix_v + xx * (1.0 - mix_v)
        xg = x * mix_g + xx * (1.0 - mix_g)
        q = xq @ Wq.T
        k = xk @ Wk.T
        v = xv @ Wv.T
        g = jax.nn.sigmoid(xg @ Wg.T)
        q_exp = jnp.exp(rmsnorm(q, norm_scale))
        k_exp = jnp.exp(rmsnorm(k, norm_scale))
        w = jnp.exp(-jnp.exp(time_decay)).reshape(H, D)
        qh = q_exp.reshape(B, T, H, D)
        kh = k_exp.reshape(B, T, H, D)
        vh = v.reshape(B, T, H, D)
        S, Z = wkv_scan(qh, kh, vh, w)
        Z_scalar = jnp.sum(qh * Z, axis=-1, keepdims=True)
        att = (S / Z_scalar).reshape(B, T, C)
        att = g * att
        return att @ Wo.T

    def _L0_attn_b_ref(hidden_states, Wq, Wk, Wv, Wo, g_weight):
        import jax, jax.numpy as jnp
        import numpy as np
        FEATURE_DIM = 16
        NUM_HEADS = 16
        HEAD_DIM = 64
        R2 = float(np.sqrt(2.0))
        RD = float(np.sqrt(FEATURE_DIM))
        RRD = float(np.sqrt(RD))
        RMS_EPS = 1e-05

        def taylor_exp(x):
            x2 = (x[..., :, None] * x[..., None, :]).reshape(*x.shape[:-1], FEATURE_DIM * FEATURE_DIM) / R2
            ones = jnp.ones_like(x[..., :1])
            return jnp.concatenate([ones, x / RRD, x2 / RD], axis=-1)

        def _reference_tuple_inner(hidden_states, Wq, Wk, Wv, Wo, g_weight):
            b, l, _ = hidden_states.shape
            q = (hidden_states @ Wq.T).reshape(b, l, NUM_HEADS, FEATURE_DIM).transpose(0, 2, 1, 3)
            k = (hidden_states @ Wk.T).reshape(b, l, NUM_HEADS, FEATURE_DIM).transpose(0, 2, 1, 3)
            v = (hidden_states @ Wv.T).reshape(b, l, NUM_HEADS, HEAD_DIM).transpose(0, 2, 1, 3)
            qf = taylor_exp(q)
            kf = taylor_exp(k)
            A_qk = jnp.einsum('bhnd,bhmd->bhnm', qf, kf)
            A_qk = jnp.tril(A_qk)
            y = jnp.einsum('bhnm,bhme->bhne', A_qk, v)
            kv_state = jnp.einsum('bhnd,bhnf->bhfd', kf, v)[:, :, None]
            rms = jax.lax.rsqrt(jnp.mean(y * y, axis=-1, keepdims=True) + RMS_EPS)
            y = y * rms * g_weight
            y = y.transpose(0, 2, 1, 3).reshape(b, l, NUM_HEADS * HEAD_DIM)
            out = y @ Wo.T
            return (out, kv_state)
        return _reference_tuple_inner(hidden_states, Wq, Wk, Wv, Wo, g_weight)[0]

    def _L0_ffn_ref(x, gate_w, gate_b, w1, b1, w2, b2):
        import jax, jax.numpy as jnp
        import numpy as np
        B, S, D, H, O, E, K = (4, 256, 128, 256, 128, 8, 2)
        logits = jnp.einsum('bsd,ed->bse', x, gate_w) + gate_b
        probs = jax.nn.softmax(logits, axis=-1)
        topk_vals, topk_idx = jax.lax.top_k(probs, K)
        h = jax.nn.relu(jnp.einsum('bsd,edh->bseh', x, w1) + b1)
        expert_out = jnp.einsum('bseh,eho->bseo', h, w2) + b2
        sel = jnp.take_along_axis(expert_out, topk_idx[..., None], axis=2)
        return jnp.sum(sel * topk_vals[..., None], axis=2)
    x = L0_attn_a_x
    x = x + _L0_attn_a_ref(_layernorm(x, axis=-1), L0_attn_a_time_decay, L0_attn_a_mix_q, L0_attn_a_mix_k, L0_attn_a_mix_v, L0_attn_a_mix_g, L0_attn_a_Wq, L0_attn_a_Wk, L0_attn_a_Wv, L0_attn_a_Wg, L0_attn_a_Wo, L0_attn_a_norm_scale)
    x = x + _L0_ffn_ref(_layernorm(x, axis=-1), L0_ffn_gate_w, L0_ffn_gate_b, L0_ffn_w1, L0_ffn_b1, L0_ffn_w2, L0_ffn_b2)
    x = x + _L0_attn_b_ref(_layernorm(x, axis=-1), L0_attn_b_Wq, L0_attn_b_Wk, L0_attn_b_Wv, L0_attn_b_Wo, L0_attn_b_g_weight)
    x = x + _L0_ffn_ref(_layernorm(x, axis=-1), L0_ffn_gate_w, L0_ffn_gate_b, L0_ffn_w1, L0_ffn_b1, L0_ffn_w2, L0_ffn_b2)
    return x

_drawn_inputs = setup_inputs


def setup_inputs(seed=0):
    import zlib

    import numpy as np

    out = dict(_drawn_inputs(seed))
    spreads = {'L0_attn_a_norm_scale': (1.0, 0.2),
     'L0_attn_b_g_weight': (1.0, 0.2),
     'L0_ffn_gate_b': (0.0, 0.1),
     'L0_ffn_b1': (0.0, 0.1),
     'L0_ffn_b2': (0.0, 0.1)}
    factors = {}
    for name, (base, spread) in spreads.items():
        noise = np.random.default_rng([zlib.crc32(name.encode()), seed]).standard_normal(out[name].shape)
        drawn = base * np.exp(spread * noise) if base else spread * noise
        out[name] = jnp.asarray(drawn.astype(out[name].dtype))
    for name, factor in factors.items():
        out[name] = (out[name] * factor).astype(out[name].dtype)
    return out
```

```python
from contextlib import ExitStack

import concourse.bass as bass
from concourse import mybir

F32 = mybir.dt.float32
F32R = mybir.dt.float32r
U8 = mybir.dt.uint8
ALU = mybir.AluOpType
ACT = mybir.ActivationFunctionType
AX_X = mybir.AxisListType.X

P = 128
B, T, C = 4, 512, 128
CH = T // P
HA, DA = 4, 32
HB, FB, DB = 16, 16, 64
GB = 4
NPAIR = HB // 2
PBUF = 3
E, HID = 8, 256
NT = E * HID // P
HBUF = 3
OUT_LAG = 2
LAGS = 4
LEVELS = range(2, 7)
LN_EPS, Q_EPS, RMS_EPS = 1e-5, 1e-8, 1e-5
LAG_AT = [0, 512, 896, 1152, 1280]

STEPS_A = ["a_stats", "a_xhat", "a_xT", "a_mix", "a_proj", "a_norm", "a_scale", "a_qkT", "a_products", "a_lags",
           "a_kends", "a_level0", "a_level1", "a_level2", "a_level3", "a_level4", "a_state", "a_y", "a_att", "a_out"]
STEPS_F = ["f_stats", "f_xhat", "f_xT", "f_logits", "f_softmax", "f_choose", "f_gT"]
STEPS_F += [f"f_tile{i}" for i in range(NT + OUT_LAG)] + ["f_out", "f_outT"]
STEPS_B = ["b_stats", "b_xhat", "b_xT", "b_qk0"] + [f"b_v{n}" for n in range(2 * CH)] + ["b_vpre", "b_s0", "b_s1"]
for _p in range(1, NPAIR + 1):
    STEPS_B += [f"b_s{2 * _p}"] if _p < NPAIR else []
    STEPS_B += [f"b_av{_p - 1}"]
    STEPS_B += [f"b_s{2 * _p + 1}"] if _p < NPAIR else []
    STEPS_B += [f"b_y{_p - 1}"]
    STEPS_B += [f"b_ss{_p - 2}"] if _p >= 2 else []
    STEPS_B += [f"b_qk{(_p + 1) // 2}"] if _p in (1, 3, 5) else []
STEPS_B += [f"b_ss{NPAIR - 1}", "b_rT"] + [f"b_rb{p}" for p in range(NPAIR + 1)] + ["b_out", "b_outT"]


def beside(one, two):
    at = [((i + 0.5) / len(one), 0, s) for i, s in enumerate(one)] + [((i + 0.5) / len(two), 1, s) for i, s in enumerate(two)]
    return [s for _, _, s in sorted(at)]


def bank_uses():
    a = [("a_xT", 0), ("a_q", 1), ("a_k", 2), ("a_v", 3), ("a_vT", 0), ("a_g", 1), ("a_qT", 2), ("a_kT", 3),
         ("a_r0", 0), ("a_r1", 1), ("a_r23", 2), ("a_den", 3), ("a_ks", 0)]
    a += [(f"a_s{i}_{h}", h) for i in range(len(LEVELS)) for h in range(HA)]
    a += [("a_u", 0), ("a_y", 1), ("a_o", 2)]
    f = [("f_xT", 6), ("f_l", 6), ("f_gT", 6)]
    for i in range(NT):
        f += [(f"f_gb{i // 2}", 6)] if i % 2 == 0 else []
        f += [(f"f_z{i}", 4 + i % 2)]
    f += [("f_o", 7), ("f_oT", 6)]
    b, ring = [], 0
    for s in STEPS_B:
        n = s[3:] if s[:3] == "b_s" and s[3:].isdigit() else None
        if n:
            new = [f"b_s{n}_{i}" for i in range(3)]
        elif s[:4] == "b_qk":
            new = [f"b_q{s[4:]}", f"b_k{s[4:]}"]
        elif s[:4] == "b_av":
            b.append((f"b_y{s[4:]}", 0))
            continue
        elif s in ("b_xT", "b_vpre"):
            b.append((s, 0))
            continue
        elif s == f"b_rb{NPAIR}":
            b.append(("b_o", 0))
            continue
        elif s[:4] in ("b_ss", "b_rb", "b_rT") or s[:3] == "b_v" or s == "b_outT":
            new = [s]
        else:
            continue
        for u in new:
            b.append((u, 1 + ring % 3))
            ring += 1
    place, count = {}, {}
    for phase in (a, f, b):
        n = [0] * 8
        for use, bank in phase:
            place[use] = (bank, n[bank])
            n[bank] += 1
        count[phase[0][0][0]] = n
    return place, count


BANK_USES, BANK_COUNT = bank_uses()

FREE_AT_1 = 4

PER = {
 'a_att': 1,
 'a_klev': 5,
 'a_kst': 1,
 'a_lagp': 4,
 'a_mv': 1,
 'a_nrm': 1,
 'a_qlev': 5,
 'a_qst': 1,
 'a_qz': 1,
 'a_rstd': 1,
 'a_ssq': 8,
 'a_states': 1,
 'a_xhat': 1,
 'a_xm': 4,
 'a_ylag': 3,
 'b_diag': 16,
 'b_j2': 16,
 'b_mv': 1,
 'b_qk_hi': 8,
 'b_rTh': 1,
 'b_rr': 8,
 'b_rstd': 1,
 'b_xh': 1,
 'b_xhat': 1,
 'b_xpre': 1,
 'b_xpreh': 1,
 'b_xprel': 1,
 'b_yn_used': 7,
 'b_ysq': 8,
 'f_ex': 1,
 'f_gTh': 1,
 'f_gate': 1,
 'f_h_used': 16,
 'f_hi': 16,
 'f_lg2': 1,
 'f_lo_even': 8,
 'f_lo_odd': 8,
 'f_mv': 1,
 'f_rstd': 1,
 'f_xh': 1,
 'f_xhat': 1,
 'step_a_dve': 7,
 'step_a_pool': 2,
 'step_b_dve': 3,
 'step_b_pool': 1,
 'step_f_dve': 13,
 'step_f_pool': 1,
}


def hybrid_block_kernel(nc: bass.Bass, a, out):
    with ExitStack() as ctx:
        def sb(name, shape, dt=F32):
            return ctx.enter_context(nc.sbuf_tensor(name, shape, dt))

        wa = {n: sb(f"wa_{n}", [P, C]) for n in "qkvgo"}
        mix = {n: sb(f"mix_{n}", [P, 1]) for n in "qkvg"}
        nscale, decay = sb("nscale", [P, 1]), sb("decay", [P, 3])
        wpow = sb("wpow", [P, P + 1])
        wrev = sb("wrev", [P, P + 1])
        w1h, w1l = sb("w1h", [P, NT, P], F32R), sb("w1l", [P, NT, P], F32R)
        w2h, w2l = sb("w2h", [P, NT, P], F32R), sb("w2l", [P, NT, P], F32R)
        b1c, nb1 = sb("b1c", [P, NT]), sb("nb1", [P, NT])
        b2r, cT, cb = sb("b2r", [E, C]), sb("cT", [P, E]), sb("cb", [E, C])
        gw, gwh, gwl = sb("gw", [P, E]), sb("gwh", [P, E], F32R), sb("gwl", [P, E], F32R)
        gbias = sb("gbias", [P, E])
        wqkh, wqkl = sb("wqkh", [P, 2 * GB, P], F32R), sb("wqkl", [P, 2 * GB, P], F32R)
        wbvh, wbvl = sb("wbvh", [P, HB * DB], F32R), sb("wbvl", [P, HB * DB], F32R)
        wbo = sb("wbo", [P, NPAIR, C])
        gcol = sb("gcol", [P, 1])
        ident, identr = sb("ident", [P, P]), sb("identr", [P, P], F32R)
        hsel = sb("hsel", [HB, NPAIR, P], F32R)
        causal = sb("causal", [P, P])
        headsum = sb("headsum", [P, P])
        pairsel = sb("pairsel", [P, 2])
        half, sgn = sb("half", [P, 1]), sb("sgn", [P, 1])
        lmask = sb("lmask", [P, len(LEVELS), 64], U8)
        mhalf, phalf = sb("mhalf", [P, 8]), sb("phalf", [P, 8])
        lneps, overc = sb("lneps", [P, CH]), sb("overc", [P, 8])
        tick, unread = sb("tick", [P, 1]), sb("unread", [P, 16])

        xs, xout = [sb("x0", [P, CH, C]), sb("x1", [P, CH, C])], sb("xout", [P, CH, C])
        norms = {}
        for ph in ("a", "f"):
            norms[ph] = {"xhat": sb(ph + "xhat", [P, CH, C]), "st6": sb(ph + "st6", [P, CH, 6]), "mv": sb(ph + "mv", [P, CH, 2]),
                         "ve": sb(ph + "ve", [P, CH]), "rstd": sb(ph + "rstd", [P, CH])}
        norms["b"] = norms["a"]
        fxh, fxl = sb("fxh", [P, T], F32R), sb("fxl", [P, T], F32R)
        bxh, bxl = sb("bxh", [P, T], F32R), sb("bxl", [P, T], F32R)

        big = sb("big", [P, 37 * T])
        bigr = sb("bigr", [P, (6 + 2 * HBUF) * T], F32R)

        def cut(at, n=1):
            return big[:, at * T:(at + n) * T]

        def cutr(at, n):
            return bigr[:, at * T:(at + n) * T].rearrange("p (j n) -> p j n", n=T)

        stage1 = cut(0, 4).rearrange("p (i n) -> p i n", i=NT)
        stage2 = cut(4, 4).rearrange("p (i n) -> p i n", i=NT)
        stageqk = cut(8, 1).rearrange("p (a n) -> p a n", a=2)
        stagewo = cut(9, 2).rearrange("p (q n) -> p q n", q=NPAIR)
        lmask_f = cut(11)[:, 0:len(LEVELS) * 64].rearrange("p (i n) -> p i n", n=64)
        stagev = cut(12, 2)

        xTs = sb("xTs", [P, T + 1])
        xdiff = cut(0)
        xm = {n: cut(1 + i) for i, n in enumerate("qkvg")}
        ssq, ms, nrm, nrme, rn = (sb(n, [P, 8]) for n in ("ssq", "ms", "nrm", "nrme", "rn"))
        qk_n = cut(6, 2).rearrange("p (a c n) -> p a c n", a=2, c=CH)
        qe, ke = cut(8), cut(9)
        vtok = cut(10).rearrange("p (c n) -> p c n", c=CH)
        vch, gth = cut(11), cut(12)
        lagp = cut(13, 3)
        squares = cut(13, 2)
        z, qz, ylag = cut(16), cut(17), cut(18)
        ytmp = cut(19, 3)
        qlev = cut(22).rearrange("p (a n) -> p a n", a=2)
        klev = sb("klev", [P, 2, T])
        qst, kst = cut(23), cut(24)
        kstT = cut(25).rearrange("p (c n) -> p c n", c=CH)
        rden, ysum, gr, att = cut(26), cut(27), cut(28), cut(29)
        pmat = sb("pmat", [P, HA, CH, P])
        state = sb("state", [P, 3, DA])
        states = sb("states", [P, 3, P])

        lg, ex, pr = sb("lg", [P, CH, E]), sb("ex", [P, CH, E]), sb("pr", [P, CH, E])
        lg2 = sb("lg2", [P, CH, E])
        m1, sm, rs1, need = sb("m1", [P, CH]), sb("sm", [P, CH]), sb("rs1", [P, CH]), sb("need", [P, CH])
        top8 = sb("top8", [P, CH, 8])
        gt, gate = sb("gt", [P, CH, E]), sb("gate", [P, CH, E])
        eq, eq2, eq4 = (sb(n, [P, CH, 2 * E]) for n in ("eq", "eq2", "eq4"))
        eq8, keep, kept = sb("eq8", [P, CH, E]), sb("keep", [P, CH, E]), sb("kept", [P, CH, E])
        both = sb("both", [P, CH, E])
        gb = [cut(30), cut(31)]
        hg = [cut(32 + i) for i in range(HBUF)]
        oT, gT = cut(35), cut(36)[0:E, :]
        hh, hl = cutr(6, HBUF), cutr(6 + HBUF, HBUF)
        gTh, gTl = sb("gTh", [E, T], F32R), sb("gTl", [E, T], F32R)

        q1, q2, kk = cutr(0, 2), cutr(2, 2), cutr(4, 2)
        ksg = sb("ksg", [P, T], F32R)
        pflat = [big[:, 4 * i * T:(4 * i + 5) * T] for i in range(PBUF)]
        vv = cut(12, 8).rearrange("p (c n) -> p c n", c=CH)
        ysb = cut(20, 8).rearrange("p (q n) -> p q n", q=NPAIR)
        ysq = [cut(28), cut(29)]
        yn, boT = [cut(0), cut(1)], cut(2)
        xsum, xpre = sb("xsum", [P, CH]), sb("xpre", [P, CH])
        xpreh, xprel = sb("xpreh", [P, CH], F32R), sb("xprel", [P, CH], F32R)
        vpre = sb("vpre", [P, NPAIR, CH])
        ssv, rr = sb("ssv", [P, NPAIR, CH, 2]), sb("rr", [P, CH, NPAIR, 2])
        rTh, rTl = bigr[0:HB, 0:T], bigr[0:HB, T:2 * T]

        bank = [ctx.enter_context(nc.psum_tensor(f"bank{i}", [P, 512], F32)) for i in range(8)]
        sems = {}

        def S(name):
            if name not in sems:
                sems[name] = ctx.enter_context(nc.semaphore("s_" + name))
            return sems[name]

        def bank_of(use):
            return bank[BANK_USES[use][0]]

        def filled(use):
            return S(f"filled{BANK_USES[use][0]}")

        def drained(use):
            return S(f"drained{BANK_USES[use][0]}")

        block = ctx.enter_context(nc.Block())

        class Count:

            def __init__(self):
                self.it, self.runs, self.given = None, {"a": (0, 0), "b": (0, 0), "f": (0, 0)}, {}

            def value(self, m, n):
                return n if self.it is None or m == 0 else self.it * m + n

            def gives(self, name):
                self.given[name] = self.given.get(name, 0) + 1
                return S(name)

            def at(self, name, n):
                per, (m, r) = PER.get(name, 1), self.runs[name[name.startswith("step_") * 5]]
                return self.value(m * per, r * per + n)

            def now(self, name):
                return self.at(name, self.given[name])

            def uses(self, use, n):
                b, k = BANK_USES[use]
                m, r = 0, k + n + (b >= FREE_AT_1)
                for phase in ("f" if use[0] == "f" else "ab"):
                    pm, pr_ = self.runs[phase]
                    m, r = m + pm * BANK_COUNT[phase][b], r + pr_ * BANK_COUNT[phase][b]
                return self.value(m, r)

            def before(self, use):
                return self.uses(use, 0)

            def before_slot(self, use):
                return self.uses(use, -BANK_USES[use][1])

            def done(self, use):
                return self.uses(use, 1)

            def end(self, phase):
                for name, n in list(self.given.items()):
                    if name[name.startswith("step_") * 5] == phase:
                        assert PER.get(name, 1) == n, (name, n)
                        del self.given[name]

        def run(k, eng, steps):

            def phase_steps(names, x, last):
                for name in names:
                    kind, n = name.rstrip("0123456789"), name[len(name.rstrip("0123456789")):]
                    if kind in steps:
                        parity = x[kind[0]]
                        steps[kind](*([int(n)] if n else []), **({"x": xs[parity], "last": last} if kind[2:] in ("stats", "xhat", "out", "outT") else {}))
                for phase in x:
                    k.end(phase)

            k.runs = {"a": (0, 0), "b": (0, 0), "f": (0, 0)}
            phase_steps(STEPS_A, {"a": 0}, False)
            with eng.Fori(0, B // 2) as it:
                k.it = it
                k.runs = {"a": (2, 1), "b": (2, 0), "f": (4, 0)}
                phase_steps(beside(STEPS_A, STEPS_F), {"a": 1, "f": 0}, False)
                k.runs = {"a": (2, 2), "b": (2, 0), "f": (4, 1)}
                phase_steps(beside(STEPS_B, STEPS_F), {"b": 0, "f": 1}, False)
                k.runs = {"a": (2, 2), "b": (2, 1), "f": (4, 2)}
                phase_steps(beside(STEPS_B, STEPS_F), {"b": 1, "f": 0}, True)
                k.runs = {"a": (2, 2), "b": (2, 2), "f": (4, 3)}
                with eng.If(it < B // 2 - 1):
                    phase_steps(beside(STEPS_A, STEPS_F), {"a": 0, "f": 1}, True)
                with eng.Else():
                    phase_steps(STEPS_F, {"f": 1}, True)
            k.it = None

        def chunks(ap):
            return ap.rearrange("p (c n) -> p c n", c=CH)

        def cs(c):
            return slice(c * P, (c + 1) * P)

        def lag_view(ap, first, n):
            return ap.rearrange("p (b l) -> p b l", l=LAGS)[:, :, first:first + n]

        def lag_part(ap, lag, base=0):
            return ap[:, LAG_AT[lag] - base:LAG_AT[lag + 1] - base].rearrange("p (b l) -> p b l", l=LAGS - lag)

        def halves(ap, j, upper):
            return ap.rearrange("p (b u n) -> p b u n", u=2, n=2 ** j)[:, :, int(upper), :]

        def f32(ap):
            return ap.bitcast(F32)

        @block.sync
        def _(sp):
            k = Count()

            def col(ap):
                return ap.rearrange("(p o) -> p o", o=1)

            def rows(ap):
                return ap.rearrange("(c p) n -> p c n", p=P)

            sp.dma_start(xs[0][:, :, :], rows(a["x"][0])).then_inc(S("x_in0"), 16)
            for n in "qkvg":
                sp.dma_start(wa[n][:, :], a[f"WaT_{n}"]).then_inc(S("wa_in"), 16)
                sp.dma_start(mix[n][:, :], a[f"mix_{n}"].rearrange("a b (p o) -> (a b p) o", o=1)).then_inc(S("wa_in"), 16)
            for dst, src in ((decay[:, 0:1], col(a["time_decay"])), (nscale[:, :], col(a["norm_scale"])), (wa["o"][:, :], a["WaT_o"])):
                sp.dma_start(dst, src).then_inc(S("wa_in"), 16)
            for dst, src in ((stage2, a["w2L"]), (b1c[:, :], a["b1T"]), (b2r[:, :], a["b2"]), (gw[:, :], a["gate_wT"]),
                             (gbias[:, :], a["gate_b"].partition_broadcast(P)), (stage1, a["w1L"]), (stageqk, a["WbqkT"]),
                             (stagev, a["WbvT"]), (stagewo, a["WboT"]),
                             (gcol[0:DB, :], col(a["g_weight"])), (gcol[DB:P, :], col(a["g_weight"]))):
                sp.dma_start(dst, src).then_inc(S("wb_in"), 16)
            sp.dma_start(xs[1][:, :, :], rows(a["x"][1])).then_inc(S("x_in1"), 16)
            for row in range(B):
                k.runs["f"] = (0, 4 * (row // 2) + 2 + row % 2)
                sp.wait_ge(drained("f_oT"), k.done("f_oT"))
                sp.dma_start(rows(out[row]), xout[:, :, :]).then_inc(S("xout_free"), 16)
                if row + 2 < B:
                    sp.dma_start(xs[row % 2][:, :, :], rows(a["x"][row + 2])).then_inc(S(f"x_in{row % 2}"), 16)
            sp.wait_ge(S("xout_free"), 16 * B + 1)

        WA_IN, WB_IN = 16 * 11, 16 * 11

        @block.gpsimd
        def _(pool):
            k = Count()
            pool.memset(ident[:, :], 0.0).then_inc(S("pool_setup"), 1)
            pool.wait_ge(S("pool_setup"), 1)
            pool.affine_select(out=ident[:, :], in_=ident[:, :], compare_op=ALU.not_equal, fill=1.0, base=0,
                               pattern=[[-1, P]], channel_multiplier=1).then_inc(S("ident"), 1)
            for t, v in ((mhalf, -0.5), (phalf, 0.5), (lneps, LN_EPS), (overc, 1.0 / C)):
                pool.memset(t[:, :], v).then_inc(S("filled_once"), 1)
            pool.memset(pmat[:, :, :, :], 0.0).then_inc(S("filled_once"), 1)
            pool.memset(klev[:, :, :], 0.0).then_inc(S("filled_once"), 1)
            pool.memset(states[:, :, :], 0.0).then_inc(S("filled_once"), 1)
            pool.memset(lmask_f, 1.0).then_inc(S("pool_setup"), 1)
            for i, j in enumerate(LEVELS):
                m = lmask_f[:, i, :].rearrange("p (b n) -> p b n", n=2 ** j)
                size = 2 ** (j + 1)
                pool.wait_ge(S("pool_setup"), 2 * i + 2)
                pool.affine_select(out=m, in_=m, compare_op=ALU.is_ge, fill=0.0, base=0,
                                   pattern=[[-size, P // size], [0, 2 ** j]], channel_multiplier=1).then_inc(S("pool_setup"), 1)
                pool.wait_ge(S("pool_setup"), 2 * i + 3)
                pool.affine_select(out=m, in_=m, compare_op=ALU.is_ge, fill=0.0, base=2 ** j - 1,
                                   pattern=[[size, P // size], [0, 2 ** j]], channel_multiplier=-1).then_inc(S("pool_setup"), 1)
            pool.memset(causal[:, :], 1.0).then_inc(S("pool_setup"), 1)
            pool.wait_ge(S("pool_setup"), 2 * len(LEVELS) + 3)
            pool.affine_select(out=causal[:, :], in_=causal[:, :], compare_op=ALU.is_ge, fill=0.0, base=0,
                               pattern=[[1, P]], channel_multiplier=-1).then_inc(S("causal"), 1)
            pool.wait_ge(S("filled_once"), 7)

            def stats(ph):
                def step(x, last):
                    n = norms[ph]
                    pool.wait_ge(S(f"{ph}_mv"), k.at(f"{ph}_mv", 1))
                    pool.tensor_tensor(n["ve"][:, :], n["mv"][:, :, 1], lneps[:, :], ALU.add).then_inc(k.gives(f"step_{ph}_pool"), 1)
                    pool.wait_ge(S(f"step_{ph}_pool"), k.now(f"step_{ph}_pool"))
                    pool.tensor_tensor(n["rstd"][:, :], n["ve"][:, :], mhalf[:, 0:CH], ALU.pow).then_inc(k.gives(f"{ph}_rstd"), 1)
                return step

            def a_norm():
                pool.wait_ge(S("a_ssq"), k.at("a_ssq", 8))
                pool.tensor_tensor(ms[:, :], ssq[:, :], overc[:, :], ALU.mult).then_inc(k.gives("step_a_pool"), 1)
                pool.wait_ge(S("step_a_pool"), k.now("step_a_pool"))
                pool.tensor_tensor(nrm[:, :], ms[:, :], phalf[:, :], ALU.pow).then_inc(k.gives("a_nrm"), 1)

            def a_klev(i):
                n = 2 ** LEVELS[i]
                if i >= 2:
                    for h in range(HA):
                        pool.wait_ge(filled(f"a_s{i - 2}_{h}"), k.done(f"a_s{i - 2}_{h}"))
                w = wrev[:, P - n:P].unsqueeze(1).broadcast_to([P, T // (2 * n), n])
                pool.tensor_tensor(halves(klev[:, i % 2, :], LEVELS[i], False), halves(ke, LEVELS[i], False), w, ALU.mult)\
                    .then_inc(k.gives("a_klev"), 1)

            def a_products():
                pool.wait_ge(drained("a_kT"), k.done("a_kT"))
                w = wrev[:, 1:P + 1].unsqueeze(1).broadcast_to([P, CH - 1, P])
                pool.tensor_tensor(chunks(kst)[:, 0:3, :], chunks(ke)[:, 0:3, :], w, ALU.mult).then_inc(k.gives("a_kst"), 1)
                a_klev(0)
                a_klev(1)

            def a_level(i):
                if i >= 1 and i + 1 < len(LEVELS):
                    a_klev(i + 1)

            def a_state():
                pool.wait_ge(drained("a_r0"), k.done("a_r0"))
                for lag in range(1, LAGS):
                    use = "a_r1" if lag == 1 else "a_r23"
                    pool.wait_ge(drained(use), k.done(use))
                    y = lag_view(ylag, lag, LAGS - lag)
                    pool.tensor_tensor(y, y, lag_part(ytmp, lag, T), ALU.add).then_inc(k.gives("a_ylag"), 1)
                    if lag < LAGS - 1:
                        pool.wait_ge(S("a_ylag"), k.at("a_ylag", lag))

            def f_tile(i):
                n = i - 1
                if n % 2 and 0 < n < NT:
                    pool.wait_ge(S("f_hi"), k.at("f_hi", n + 1))
                    if n >= HBUF:
                        pool.wait_ge(S("f_h_used"), k.at("f_h_used", n - HBUF + 1))
                    pool.tensor_tensor(hl[:, n % HBUF, :], hg[n % HBUF], f32(hh[:, n % HBUF, :]), ALU.subtract)\
                        .then_inc(k.gives("f_lo_odd"), 1)

            def b_ss(p):
                pool.wait_ge(drained(f"b_ss{p}"), k.done(f"b_ss{p}"))
                pool.tensor_tensor(rr[:, :, p, :], ssv[:, p, :, :], mhalf[:, :].rearrange("p (c a) -> p c a", a=2), ALU.pow)\
                    .then_inc(k.gives("b_rr"), 1)

            run(k, pool, {"a_stats": stats("a"), "b_stats": stats("b"), "f_stats": stats("f"), "a_norm": a_norm,
                          "a_products": a_products, "a_level": a_level, "a_state": a_state, "f_tile": f_tile, "b_ss": b_ss})

        @block.scalar
        def _(act):
            k = Count()
            act.wait_ge(S("wa_in"), WA_IN)
            act.activation(decay[:, 1:2], decay[:, 0:1], ACT.Exp).then_inc(S("exp_decay"), 1)
            act.wait_ge(S("exp_decay"), 1)
            act.activation(decay[:, 2:3], decay[:, 1:2], ACT.Exp, scale=-1.0).then_inc(S("w"), 1)
            act.wait_ge(S("wb_in"), WB_IN)
            act.activation(w1h[:, :, :], stage1, ACT.Copy).then_inc(S("w_hi"), 1)
            act.activation(w2h[:, :, :], stage2, ACT.Copy).then_inc(S("w_hi"), 1)
            act.activation(wbvh[:, :], stagev, ACT.Copy).then_inc(S("w_hi"), 1)
            act.activation(gwh[:, :], gw[:, :], ACT.Copy).then_inc(S("w_hi"), 1)
            dst = wqkh[:, :, :].rearrange("p g (h u f) -> p (g h) u f", u=2, f=FB)
            src = stageqk.rearrange("p a (h f) -> p (a h) f", f=FB)
            for u in range(2):
                act.activation(dst[:, :, u, :], src, ACT.Copy).then_inc(S("w_hi"), 1)
            act.wait_ge(S("cT_full"), 1)
            act.activation(cT[:, :], bank[0][:, 0:E], ACT.Copy).then_inc(S("cT"), 1)

            def a_xT():
                act.wait_ge(filled("a_xT"), k.done("a_xT"))
                act.activation(xTs[:, 1:T + 1], bank_of("a_xT")[:, :], ACT.Copy).then_inc(drained("a_xT"), 1)

            def a_proj():
                for i, n in enumerate("qk"):
                    act.wait_ge(filled(f"a_{n}"), k.done(f"a_{n}"))
                    for c in range(CH):
                        act.activation(squares[:, (i * CH + c) * P:(i * CH + c + 1) * P], bank_of(f"a_{n}")[:, cs(c)], ACT.Square,
                                       accum_out=ssq[:, i * CH + c:i * CH + c + 1]).then_inc(k.gives("a_ssq"), 1)
                act.wait_ge(filled("a_v"), k.done("a_v"))
                act.activation(vtok.rearrange("p c n -> p (c n)"), bank_of("a_v")[:, :], ACT.Copy).then_inc(drained("a_v"), 1)
                act.wait_ge(filled("a_vT"), k.done("a_vT"))
                act.activation(vch, bank_of("a_vT")[:, :], ACT.Copy).then_inc(drained("a_vT"), 1)

            def a_qkT():
                act.wait_ge(filled("a_qT"), k.done("a_qT"))
                act.activation(qe, bank_of("a_qT")[:, :], ACT.Exp, scale=nscale[:, :]).then_inc(drained("a_qT"), 1)
                act.wait_ge(filled("a_kT"), k.done("a_kT"))
                act.activation(ke, bank_of("a_kT")[:, :], ACT.Exp, scale=nscale[:, :]).then_inc(drained("a_kT"), 1)
                act.wait_ge(filled("a_g"), k.done("a_g"))
                act.activation(gth, bank_of("a_g")[:, :], ACT.Tanh, scale=0.5).then_inc(drained("a_g"), 1)

            def a_kends():
                act.wait_ge(filled("a_ks"), k.done("a_ks"))
                act.activation(kstT[:, 0:3, :].rearrange("p c n -> p (c n)"), bank_of("a_ks")[:, 0:3 * P], ACT.Copy)\
                    .then_inc(drained("a_ks"), 1)

            def hi_of_x(use, dst, name):
                act.wait_ge(filled(use), k.done(use))
                act.activation(dst[:, :], bank_of(use)[:, :], ACT.Copy).then_inc(k.gives(name), 1)

            def f_softmax():
                act.wait_ge(S("f_lg2"), k.at("f_lg2", 1))
                act.activation(ex[:, :, :], lg2[:, :, :], ACT.Exp).then_inc(k.gives("f_ex"), 1)

            def f_gT():
                act.wait_ge(filled("f_gT"), k.done("f_gT"))
                act.activation(gT, bank_of("f_gT")[0:E, :], ACT.Copy)
                act.activation(gTh[:, :], bank_of("f_gT")[0:E, :], ACT.Copy).then_inc(k.gives("f_gTh"), 1)

            def f_tile(i):
                if i < NT and i % 2 == 0:
                    e = i // 2
                    act.wait_ge(filled(f"f_gb{e}"), k.done(f"f_gb{e}"))
                    if e >= 2:
                        act.wait_ge(drained(f"f_z{2 * e - 3}"), k.done(f"f_z{2 * e - 3}"))
                    act.activation(gb[e % 2], bank_of(f"f_gb{e}")[:, :], ACT.Copy).then_inc(drained(f"f_gb{e}"), 1)
                n = i - 1
                if 0 <= n < NT:
                    act.wait_ge(drained(f"f_z{n}"), k.done(f"f_z{n}"))
                    if n >= HBUF:
                        act.wait_ge(S("f_h_used"), k.at("f_h_used", n - HBUF + 1))
                    act.activation(hh[:, n % HBUF, :], hg[n % HBUF], ACT.Copy).then_inc(k.gives("f_hi"), 1)

            def f_out(x, last):
                act.wait_ge(filled("f_o"), k.done("f_o"))
                act.activation(oT, bank_of("f_o")[:, :], ACT.Copy).then_inc(drained("f_o"), 1)

            def b_qk(g):
                if g >= 2:
                    use = f"b_s{4 * g - 5}_2"
                    act.wait_ge(filled(use), k.done(use))
                act.wait_ge(filled(f"b_q{g}"), k.done(f"b_q{g}"))
                act.activation(q1[:, g % 2, :], bank_of(f"b_q{g}")[:, :], ACT.Copy).then_inc(k.gives("b_qk_hi"), 1)
                act.wait_ge(filled(f"b_k{g}"), k.done(f"b_k{g}"))
                if g >= 1:
                    act.wait_ge(drained(f"b_k{g - 1}"), k.done(f"b_k{g - 1}"))
                act.activation(ksg[:, :], bank_of(f"b_k{g}")[:, :], ACT.Copy, scale=sgn[:, :]).then_inc(k.gives("b_qk_hi"), 1)

            def b_v(n):
                if n % 2 == 0:
                    act.wait_ge(filled(f"b_v{n}"), k.done(f"b_v{n}"))
                    act.activation(vv[:, n // 2, 0:512], bank_of(f"b_v{n}")[:, :], ACT.Copy).then_inc(drained(f"b_v{n}"), 1)

            def b_vpre():
                act.wait_ge(S("b_xpre"), k.at("b_xpre", 1))
                act.activation(xpreh[:, :], xpre[:, :], ACT.Copy).then_inc(k.gives("b_xpreh"), 1)
                act.wait_ge(filled("b_vpre"), k.done("b_vpre"))
                act.activation(vpre[:, :, :].rearrange("p q c -> p (q c)"), bank_of("b_vpre")[:, 0:NPAIR * CH], ACT.Copy)\
                    .then_inc(drained("b_vpre"), 1)

            def b_s(h):
                if h >= PBUF:
                    use = f"b_y{(h - PBUF) // 2}"
                    act.wait_ge(filled(use), k.done(use))
                for j in range(CH):
                    use = f"b_s{h}_{min(j, 2)}"
                    if j < 3:
                        act.wait_ge(filled(use), k.done(use))
                    at = 2 * P if j == 3 else 0
                    act.activation(pflat[h % PBUF][:, j * (T + P):(j + 1) * T], bank_of(use)[:, at:at + T - j * P], ACT.Square,
                                   bias=1.0, scale=0.25).then_inc(k.gives("b_j2") if j == 2 else drained(use), 1)

            def b_y(p):
                act.wait_ge(drained(f"b_y{p}"), k.done(f"b_y{p}"))
                if p >= 2:
                    act.wait_ge(filled(f"b_ss{p - 2}"), k.done(f"b_ss{p - 2}"))
                act.activation(ysq[p % 2], ysb[:, p, :], ACT.Square).then_inc(k.gives("b_ysq"), 1)

            def b_rT():
                act.wait_ge(filled("b_rT"), k.done("b_rT"))
                act.activation(rTh, bank_of("b_rT")[0:HB, :], ACT.Copy).then_inc(k.gives("b_rTh"), 1)

            def b_out(x, last):
                act.wait_ge(filled("b_o"), k.done("b_o"))
                act.activation(boT, bank_of("b_o")[:, :], ACT.Copy).then_inc(drained("b_o"), 1)

            run(k, act, {"a_xT": a_xT, "a_proj": a_proj, "a_qkT": a_qkT, "a_kends": a_kends,
                         "f_xT": lambda: hi_of_x("f_xT", fxh, "f_xh"), "f_softmax": f_softmax, "f_gT": f_gT, "f_tile": f_tile, "f_out": f_out,
                         "b_xT": lambda: hi_of_x("b_xT", bxh, "b_xh"), "b_qk": b_qk, "b_v": b_v, "b_vpre": b_vpre, "b_s": b_s, "b_y": b_y,
                         "b_rT": b_rT, "b_out": b_out})

        @block.tensor
        def _(pe):
            k = Count()
            mm = pe.matmul
            pe.wait_ge(S("wb_in"), WB_IN)
            pe.wait_ge(S("ident"), 1)
            for i in range(NT):
                ins = mm(bank[0][:, i // 2:i // 2 + 1], stage2[:, i, :], b1c[:, i:i + 1], start=(i % 2 == 0), stop=(i % 2 == 1))
            ins.then_inc(S("cT_full"), 1)
            pe.wait_ge(S("cT"), 1)
            pe.transpose(bank[1][0:E, 0:C], cT[:, :], ident[:, :]).then_inc(S("cb_full"), 1)
            pe.wait_ge(S("setup_done"), 1)

            def transposes(use, src, n=P, count=CH):
                pe.wait_ge(drained(use), k.before(use))
                for c in range(count):
                    ins = pe.transpose(bank_of(use)[0:n, cs(c)], src(c), ident[:, :])
                ins.then_inc(filled(use), 1)

            def three(o, lhs, rhs, start=True, stop=True):
                mm(o, lhs[0], rhs[0], start=start, stop=False)
                mm(o, lhs[0], rhs[1], start=False, stop=False)
                return mm(o, lhs[1], rhs[0], start=False, stop=stop)

            def a_xT():
                pe.wait_ge(S("a_xhat"), k.at("a_xhat", 1))
                transposes("a_xT", lambda c: norms["a"]["xhat"][:, c, :])

            def a_proj():
                for i, n in enumerate("qkv"):
                    pe.wait_ge(S("a_xm"), k.at("a_xm", i + 1))
                    pe.wait_ge(drained(f"a_{n}"), k.before(f"a_{n}"))
                    for c in range(CH):
                        ins = mm(bank_of(f"a_{n}")[:, cs(c)], xm[n][:, cs(c)], wa[n][:, :], start=True, stop=True)
                    ins.then_inc(filled(f"a_{n}"), 1)
                pe.wait_ge(drained("a_vT"), k.before("a_vT"))
                mm(bank_of("a_vT")[:, :], wa["v"][:, :], xm["v"], start=True, stop=True).then_inc(filled("a_vT"), 1)

            def a_scale():
                pe.wait_ge(S("a_xm"), k.at("a_xm", 4))
                pe.wait_ge(drained("a_g"), k.before("a_g"))
                mm(bank_of("a_g")[:, :], wa["g"][:, :], xm["g"], start=True, stop=True).then_inc(filled("a_g"), 1)

            def a_qkT():
                for i, n in enumerate("qk"):
                    pe.wait_ge(drained(f"a_{n}"), k.done(f"a_{n}"))
                    transposes(f"a_{n}T", lambda c: qk_n[:, i, c, :])

            def a_lags():
                for lag, use in enumerate(("a_r0", "a_r1", "a_r23", "a_r23")):
                    pe.wait_ge(S("a_lagp"), k.at("a_lagp", lag + 1))
                    if lag < 3:
                        pe.wait_ge(drained(use), k.before(use))
                    at, n = (256 if lag == 3 else 0), LAG_AT[lag + 1] - LAG_AT[lag]
                    ins = mm(bank_of(use)[:, at:at + n], headsum[:, :], lagp[:, LAG_AT[lag]:LAG_AT[lag + 1]], start=True, stop=True)
                    if lag != 2:
                        ins.then_inc(filled(use), 1)
                pe.wait_ge(S("a_qz"), k.at("a_qz", 1))
                pe.wait_ge(drained("a_den"), k.before("a_den"))
                mm(bank_of("a_den")[:, :], headsum[:, :], qz, start=True, stop=True).then_inc(filled("a_den"), 1)

            def a_kends():
                pe.wait_ge(S("a_kst"), k.at("a_kst", 1))
                transposes("a_ks", lambda c: kst[:, cs(c)], count=3)

            def a_level(i):
                pe.wait_ge(S("a_klev"), k.at("a_klev", i + 1))
                pe.wait_ge(S("a_qlev"), k.at("a_qlev", i + 1))
                for h in range(HA):
                    pe.wait_ge(drained(f"a_s{i}_{h}"), k.before(f"a_s{i}_{h}"))
                for c in range(CH):
                    for h in range(HA):
                        use, r = f"a_s{i}_{h}", slice(32 * h, 32 * h + 32)
                        ins = mm(bank_of(use)[:, c * 64:(c + 1) * 64], klev[r, i % 2, cs(c)], qlev[r, i % 2, c * 64:(c + 1) * 64],
                                 start=True, stop=True)
                        if c == CH - 1:
                            ins.then_inc(filled(use), 1)

            def a_state():
                pe.wait_ge(drained("a_ks"), k.done("a_ks"))
                pe.wait_ge(drained("a_u"), k.before("a_u"))
                for c in range(3):
                    for h in range(HA):
                        r = slice(32 * h, 32 * h + 32)
                        ins = mm(bank_of("a_u")[r, c * DA:(c + 1) * DA], kstT[:, c, r], vtok[:, c, r], start=True, stop=True)
                ins.then_inc(filled("a_u"), 1)

            def a_y():
                pe.wait_ge(S("a_states"), k.at("a_states", 1))
                pe.wait_ge(S("a_qst"), k.at("a_qst", 1))
                for h in range(HA):
                    pe.wait_ge(drained(f"a_s{len(LEVELS) - 1}_{h}"), k.done(f"a_s{len(LEVELS) - 1}_{h}"))
                pe.wait_ge(drained("a_y"), k.before("a_y"))
                for c in range(CH):
                    if c:
                        mm(bank_of("a_y")[:, cs(c)], states[:, c - 1, :], qst[:, cs(c)], start=True, stop=False)
                    for h in range(HA):
                        r = slice(32 * h, 32 * h + 32)
                        ins = mm(bank_of("a_y")[r, cs(c)], vtok[:, c, r], pmat[:, h, c, :], start=(c == 0), stop=True)
                ins.then_inc(filled("a_y"), 1)

            def a_out(x, last):
                pe.wait_ge(S("a_att"), k.at("a_att", 1))
                pe.wait_ge(drained("a_o"), k.before("a_o"))
                for c in range(CH):
                    ins = mm(bank_of("a_o")[:, cs(c)], att[:, cs(c)], wa["o"][:, :], start=True, stop=True)
                ins.then_inc(filled("a_o"), 1)

            def f_xT():
                pe.wait_ge(S("f_xhat"), k.at("f_xhat", 1))
                transposes("f_xT", lambda c: norms["f"]["xhat"][:, c, :])

            def f_logits():
                pe.wait_ge(drained("f_xT"), k.done("f_xT"))
                pe.wait_ge(drained("f_l"), k.before("f_l"))
                for c in range(CH):
                    ins = three(bank_of("f_l")[:, c * E:(c + 1) * E], (fxh[:, cs(c)], fxl[:, cs(c)]), (gwh[:, :], gwl[:, :]))
                ins.then_inc(filled("f_l"), 1)

            def f_gT():
                pe.wait_ge(S("f_gate"), k.at("f_gate", 1))
                transposes("f_gT", lambda c: gate[:, c, :], E)

            def f_tile(i):
                if i < NT:
                    if i % 2 == 0:
                        use, one = f"f_gb{i // 2}", identr[0:E, i // 2:i // 2 + 1].broadcast_to([E, P])
                        if i == 0:
                            pe.wait_ge(drained("f_gT"), k.done("f_gT"))
                        pe.wait_ge(drained(use), k.before(use))
                        mm(bank_of(use)[:, :], one, gTh[:, :], start=True, stop=False)
                        mm(bank_of(use)[:, :], one, gTl[:, :], start=False, stop=True).then_inc(filled(use), 1)
                    use = f"f_z{i}"
                    pe.wait_ge(drained(use), k.before(use))
                    three(bank_of(use)[:, :], (w1h[:, i, :], w1l[:, i, :]), (fxh[:, :], fxl[:, :])).then_inc(filled(use), 1)
                n = i - OUT_LAG
                if n >= 0:
                    pe.wait_ge(S("f_hi"), k.at("f_hi", n + 1))
                    lo = ("f_lo_even", "f_lo_odd")[n % 2]
                    pe.wait_ge(S(lo), k.at(lo, n // 2 + 1))
                    if n == 0:
                        pe.wait_ge(drained("f_o"), k.before("f_o"))
                    three(bank_of("f_o")[:, :], (w2h[:, n, :], w2l[:, n, :]), (hh[:, n % HBUF, :], hl[:, n % HBUF, :]),
                          start=(n == 0), stop=False).then_inc(k.gives("f_h_used"), 1)

            def f_out(x, last):
                mm(bank_of("f_o")[:, :], cb[:, :], gT, start=False, stop=True).then_inc(filled("f_o"), 1)

            def f_outT(x, last):
                pe.wait_ge(drained("f_o"), k.done("f_o"))
                transposes("f_oT", lambda c: oT[:, cs(c)])

            def b_xT():
                pe.wait_ge(S("b_xhat"), k.at("b_xhat", 1))
                transposes("b_xT", lambda c: norms["b"]["xhat"][:, c, :])

            def b_qk(g):
                if g == 0:
                    pe.wait_ge(drained("b_xT"), k.done("b_xT"))
                for i, use in enumerate((f"b_q{g}", f"b_k{g}")):
                    w = i * GB + g
                    pe.wait_ge(drained(use), k.before(use))
                    three(bank_of(use)[:, :], (wqkh[:, w, :], wqkl[:, w, :]), (bxh[:, :], bxl[:, :])).then_inc(filled(use), 1)

            def b_v(n):
                use, w = f"b_v{n}", slice(n % 2 * 512, n % 2 * 512 + 512)
                pe.wait_ge(drained(use), k.before(use))
                three(bank_of(use)[:, :], (bxh[:, cs(n // 2)], bxl[:, cs(n // 2)]), (wbvh[:, w], wbvl[:, w])).then_inc(filled(use), 1)

            def b_vpre():
                pe.wait_ge(S("b_xprel"), k.at("b_xprel", 1))
                pe.wait_ge(drained("b_vpre"), k.before("b_vpre"))
                for p in range(NPAIR):
                    ins = three(bank_of("b_vpre")[:, p * CH:(p + 1) * CH], (wbvh[:, cs(p)], wbvl[:, cs(p)]), (xpreh[:, :], xprel[:, :]))
                ins.then_inc(filled("b_vpre"), 1)

            def b_s(h):
                g, r = h // 4, slice(h % 4 * 32, h % 4 * 32 + 32)
                if h % 4 == 0:
                    pe.wait_ge(drained(f"b_q{g}"), k.done(f"b_q{g}"))
                    pe.wait_ge(drained(f"b_k{g}"), k.done(f"b_k{g}"))
                for j in range(CH):
                    use = f"b_s{h}_{min(j, 2)}"
                    if j < 3:
                        pe.wait_ge(drained(use), k.before(use))
                    at = 2 * P if j == 3 else 0
                    o, w = bank_of(use)[:, at:at + T - j * P], kk[r, g % 2, cs(j)]
                    mm(o, w, q1[r, g % 2, j * P:T], start=True, stop=False)
                    ins = mm(o, w, q2[r, g % 2, j * P:T], start=False, stop=True)
                    if j != 2:
                        ins.then_inc(filled(use), 1)

            def b_av(p):
                if p == 0:
                    for n in range(2 * CH - 3, 2 * CH):
                        pe.wait_ge(drained(f"b_v{n}"), k.done(f"b_v{n}"))
                use = f"b_y{p}"
                pe.wait_ge(S("b_diag"), k.at("b_diag", 2 * p + 2))
                pe.wait_ge(drained(use), k.before(use))
                for j in range(CH):
                    for u in range(2):
                        h = 2 * p + u
                        ins = mm(bank_of(use)[DB * u:DB * u + DB, j * P:T], vv[:, j, h * DB:(h + 1) * DB],
                                 pflat[h % PBUF][:, j * (T + P):(j + 1) * T], start=(j == 0), stop=(j == CH - 1))
                ins.then_inc(filled(use), 1)

            def b_ss(p):
                pe.wait_ge(S("b_ysq"), k.at("b_ysq", p + 1))
                pe.wait_ge(drained(f"b_ss{p}"), k.before(f"b_ss{p}"))
                for c in range(CH):
                    ins = mm(bank_of(f"b_ss{p}")[:, 2 * c:2 * c + 2], ysq[p % 2][:, cs(c)], pairsel[:, :], start=True, stop=True)
                ins.then_inc(filled(f"b_ss{p}"), 1)

            def b_rT():
                pe.wait_ge(S("b_rr"), k.at("b_rr", NPAIR))
                transposes("b_rT", lambda c: rr[:, c, :, :].rearrange("p q a -> p (q a)"), HB)

            def b_rb(p):
                if p < NPAIR:
                    use = f"b_rb{p}"
                    if p == 0:
                        pe.wait_ge(drained("b_rT"), k.done("b_rT"))
                    pe.wait_ge(drained(use), k.before(use))
                    mm(bank_of(use)[:, :], hsel[:, p, :], rTh, start=True, stop=False)
                    mm(bank_of(use)[:, :], hsel[:, p, :], rTl, start=False, stop=True).then_inc(filled(use), 1)
                if p >= 1:
                    pe.wait_ge(drained(f"b_rb{p - 1}"), k.done(f"b_rb{p - 1}"))
                    if p == 1:
                        pe.wait_ge(drained("b_o"), k.before("b_o"))
                    ins = mm(bank_of("b_o")[:, :], wbo[:, p - 1, :], yn[(p - 1) % 2], start=(p == 1), stop=(p == NPAIR))
                    ins.then_inc(filled("b_o") if p == NPAIR else k.gives("b_yn_used"), 1)

            def b_outT(x, last):
                pe.wait_ge(drained("b_o"), k.done("b_o"))
                transposes("b_outT", lambda c: boT[:, cs(c)])

            run(k, pe, {"a_xT": a_xT, "a_proj": a_proj, "a_scale": a_scale, "a_qkT": a_qkT, "a_lags": a_lags, "a_kends": a_kends,
                        "a_level": a_level, "a_state": a_state, "a_y": a_y, "a_out": a_out,
                        "f_xT": f_xT, "f_logits": f_logits, "f_gT": f_gT, "f_tile": f_tile, "f_out": f_out, "f_outT": f_outT,
                        "b_xT": b_xT, "b_qk": b_qk, "b_v": b_v, "b_vpre": b_vpre, "b_s": b_s, "b_av": b_av, "b_ss": b_ss, "b_rT": b_rT,
                        "b_rb": b_rb, "b_outT": b_outT})

        @block.vector
        def _(dve):
            k = Count()
            tt, ts, stt, copy = dve.tensor_tensor, dve.tensor_scalar, dve.scalar_tensor_tensor, dve.tensor_copy
            setup = [0]

            def settled(ins):
                setup[0] += 1
                ins.then_inc(S("dve_setup"), 1)
                dve.wait_ge(S("dve_setup"), setup[0])

            dve.memset(headsum[:, :], 0.0)
            settled(dve.memset(pairsel[:, :], 0.0))
            for h in range(HA):
                r = slice(32 * h, 32 * h + 32)
                dve.memset(headsum[r, r], 1.0)
            dve.memset(pairsel[0:64, 0:1], 1.0)
            dve.memset(pairsel[64:P, 1:2], 1.0)
            dve.memset(xTs[:, 0:1], 0.0)
            dve.memset(xpre[:, 0:1], 0.0)
            for t in (eq, eq2, eq4):
                dve.memset(t[:, :, 0:E], 0.0)
            for i in range(FREE_AT_1, 8):
                dve.memset(unread[:, i:i + 1], 0.0).then_inc(S(f"drained{i}"), 1)
                dve.memset(unread[:, 8 + i:9 + i], 0.0).then_inc(S(f"filled{i}"), 1)
            dve.memset(unread[:, 0:1], 0.0).then_inc(S("xout_free"), 1)
            dve.memset(wpow[:, 0:1], 1.0)
            settled(dve.memset(wrev[:, P:P + 1], 1.0))
            dve.wait_ge(S("ident"), 1)
            copy(identr[:, :], ident[:, :])
            copy(hsel[:, :, :].rearrange("h q (u n) -> h (q u) n", u=2), ident[0:HB, 0:HB].unsqueeze(2).broadcast_to([HB, HB, DB]))
            settled(dve.tensor_reduce(half[:, :], ident[:, :].rearrange("p (a u f) -> p a u f", u=2, f=FB)[:, :, 1, :],
                                      mybir.AxisListType.XY, ALU.add))
            ts(sgn[:, :], half[:, :], 2.0, -1.0, ALU.mult, ALU.add)
            dve.wait_ge(S("pool_setup"), 2 * len(LEVELS) + 2)
            copy(lmask[:, :, :], lmask_f)
            dve.wait_ge(S("w"), 1)
            copy(wpow[:, 1:2], decay[:, 2:3])
            settled(copy(wrev[:, P - 1:P], decay[:, 2:3]))
            n = 1
            while n < P:
                w = wpow[:, n:n + 1]
                ts(wpow[:, n + 1:2 * n + 1], wpow[:, 1:n + 1], w, None, ALU.mult)
                settled(ts(wrev[:, P - 2 * n:P - n], wrev[:, P - n:P], w, None, ALU.mult))
                n *= 2
            dve.wait_ge(S("wb_in"), WB_IN)
            ts(nb1[:, :], b1c[:, :], -1.0, None, ALU.mult)
            ts(wbo[:, :, :], stagewo, gcol[:, :], None, ALU.mult)
            dve.wait_ge(S("w_hi"), 6)
            tt(w1l[:, :, :], stage1, f32(w1h[:, :, :]), ALU.subtract)
            tt(w2l[:, :, :], stage2, f32(w2h[:, :, :]), ALU.subtract)
            tt(wbvl[:, :], stagev, f32(wbvh[:, :]), ALU.subtract)
            tt(gwl[:, :], gw[:, :], f32(gwh[:, :]), ALU.subtract)
            hi = wqkh[:, :, :].rearrange("p g (h u f) -> p (g h) u f", u=2, f=FB)
            lo = wqkl[:, :, :].rearrange("p g (h u f) -> p (g h) u f", u=2, f=FB)
            src = stageqk.rearrange("p a (h f) -> p (a h) f", f=FB)
            for u in range(2):
                tt(lo[:, :, u, :], src, f32(hi[:, :, u, :]), ALU.subtract)
            dve.wait_ge(S("cb_full"), 1)
            tt(cb[:, :], bank[1][0:E, 0:C], b2r[:, :], ALU.add).then_inc(S("setup_done"), 1)
            dve.wait_ge(S("causal"), 1)

            def stats(ph):
                def step(x, last):
                    n = norms[ph]
                    if ph == "a":
                        odd = x is xs[1]
                        dve.wait_ge(S(f"x_in{int(odd)}"), k.value(16, 16 if odd else 32) if k.it is not None else 16)
                    else:
                        use = "f_oT" if ph == "b" else "b_outT" if last else "a_o"
                        dve.wait_ge(drained(use), k.before_slot(use))
                    for c in range(CH):
                        ins = dve.bn_stats(n["st6"][:, c, :], x[:, c, :])
                    ins.then_inc(k.gives(f"step_{ph}_dve"), 1)
                    dve.wait_ge(S(f"step_{ph}_dve"), k.now(f"step_{ph}_dve"))
                    dve.memset(tick[:, :], 0.0)
                    for c in range(CH):
                        ins = dve.bn_aggr(n["mv"][:, c, :], n["st6"][:, c, :])
                    ins.then_inc(k.gives(f"{ph}_mv"), 1)
                return step

            def xhat(ph):
                def step(x, last):
                    n = norms[ph]
                    dve.wait_ge(S(f"{ph}_rstd"), k.at(f"{ph}_rstd", 1))
                    for c in range(CH):
                        ins = ts(n["xhat"][:, c, :], x[:, c, :], n["mv"][:, c, 0:1], n["rstd"][:, c:c + 1], ALU.subtract, ALU.mult)
                    ins.then_inc(k.gives(f"{ph}_xhat"), 1)
                return step

            def a_mix():
                dve.wait_ge(drained("a_xT"), k.done("a_xT"))
                tt(xdiff, xTs[:, 1:T + 1], xTs[:, 0:T], ALU.subtract).then_inc(k.gives("step_a_dve"), 1)
                dve.wait_ge(S("step_a_dve"), k.now("step_a_dve"))
                for n in "qkvg":
                    stt(xm[n], xdiff, mix[n][:, :], xTs[:, 0:T], ALU.mult, ALU.add).then_inc(k.gives("a_xm"), 1)

            def a_scale():
                dve.wait_ge(S("a_nrm"), k.at("a_nrm", 1))
                ts(nrme[:, :], nrm[:, :], Q_EPS, None, ALU.add).then_inc(k.gives("step_a_dve"), 1)
                dve.wait_ge(S("step_a_dve"), k.now("step_a_dve"))
                dve.reciprocal(rn[:, :], nrme[:, :]).then_inc(k.gives("step_a_dve"), 1)
                dve.wait_ge(S("step_a_dve"), k.now("step_a_dve"))
                for i, n in enumerate("qk"):
                    for c in range(CH):
                        ins = ts(qk_n[:, i, c, :], bank_of(f"a_{n}")[:, cs(c)], rn[:, i * CH + c:i * CH + c + 1], None, ALU.mult)
                    ins.then_inc(drained(f"a_{n}"), 1)

            def a_products():
                dve.wait_ge(drained("a_qT"), k.done("a_qT"))
                dve.wait_ge(drained("a_kT"), k.done("a_kT"))
                for lag in range(LAGS):
                    n = LAGS - lag
                    stt(lag_part(lagp, lag), lag_view(ke, 0, n), wpow[:, lag:lag + 1], lag_view(qe, lag, n), ALU.mult, ALU.mult)\
                        .then_inc(k.gives("a_lagp"), 1)
                dve.tensor_tensor_scan(z, wpow[:, 1:2].broadcast_to([P, T]), ke, 0.0, ALU.mult, ALU.add).then_inc(k.gives("step_a_dve"), 1)
                dve.wait_ge(S("step_a_dve"), k.now("step_a_dve"))
                tt(qz, qe, z, ALU.mult).then_inc(k.gives("a_qz"), 1)
                q_level(0)
                q_level(1)

            def q_level(i):
                n = 2 ** LEVELS[i]
                if i >= 2:
                    for h in range(HA):
                        dve.wait_ge(filled(f"a_s{i - 2}_{h}"), k.done(f"a_s{i - 2}_{h}"))
                w = wpow[:, 0:n].unsqueeze(1).broadcast_to([P, T // (2 * n), n])
                o = qlev[:, i % 2, :].rearrange("p (b n) -> p b n", n=n)
                tt(o, halves(qe, LEVELS[i], True), w, ALU.mult).then_inc(k.gives("a_qlev"), 1)

            def a_lags():
                dve.wait_ge(drained("a_vT"), k.done("a_vT"))
                dve.wait_ge(filled("a_r0"), k.done("a_r0"))
                tt(ylag, bank_of("a_r0")[:, :], vch, ALU.mult).then_inc(drained("a_r0"), 1)
                for lag, at, use in ((1, 0, "a_r1"), (2, 0, "a_r23"), (3, 256, "a_r23")):
                    if lag < 3:
                        dve.wait_ge(filled(use), k.done(use))
                    n = LAGS - lag
                    ins = tt(lag_part(ytmp, lag, T), bank_of(use)[:, at:at + n * P].rearrange("p (b l) -> p b l", l=n), lag_view(vch, 0, n), ALU.mult)
                    if lag != 2:
                        ins.then_inc(drained(use), 1)
                dve.wait_ge(filled("a_den"), k.done("a_den"))
                dve.reciprocal(rden, bank_of("a_den")[:, :]).then_inc(drained("a_den"), 1)

            def a_kends():
                w = wpow[:, 1:P + 1].unsqueeze(1).broadcast_to([P, CH - 1, P])
                tt(chunks(qst)[:, 1:, :], chunks(qe)[:, 1:, :], w, ALU.mult).then_inc(k.gives("a_qst"), 1)

            def a_level(i):
                n = 2 ** LEVELS[i]
                for h in range(HA):
                    dve.wait_ge(filled(f"a_s{i}_{h}"), k.done(f"a_s{i}_{h}"))
                dve.memset(tick[:, :], 0.0)
                for h in range(HA):
                    o = pmat[:, h, :, :].rearrange("p c (b u n) -> p c b u n", u=2, n=n)[:, :, :, 1, :]
                    m = lmask[:, i, :].rearrange("p (b n) -> p b n", n=n).unsqueeze(1).broadcast_to([P, CH, 64 // n, n])
                    d = bank_of(f"a_s{i}_{h}")[:, 0:CH * 64].rearrange("p (c b n) -> p c b n", c=CH, n=n)
                    dve.copy_predicated(o, m, d).then_inc(drained(f"a_s{i}_{h}"), 1)
                if i + 2 < len(LEVELS):
                    q_level(i + 2)

            def a_state():
                dve.wait_ge(filled("a_u"), k.done("a_u"))
                u3 = bank_of("a_u")[:, 0:3 * DA].rearrange("p (c n) -> p c n", c=3)
                copy(state[:, 0, :], u3[:, 0, :]).then_inc(k.gives("step_a_dve"), 1)
                dve.wait_ge(S("step_a_dve"), k.now("step_a_dve"))
                stt(state[:, 1, :], state[:, 0, :], wpow[:, P:P + 1], u3[:, 1, :], ALU.mult, ALU.add).then_inc(k.gives("step_a_dve"), 1)
                dve.wait_ge(S("step_a_dve"), k.now("step_a_dve"))
                stt(state[:, 2, :], state[:, 1, :], wpow[:, P:P + 1], u3[:, 2, :], ALU.mult, ALU.add).then_inc(drained("a_u"), 1)
                dve.wait_ge(drained("a_u"), k.done("a_u"))
                for h in range(HA):
                    r = slice(32 * h, 32 * h + 32)
                    ins = copy(states[r, :, r], state[r, :, :])
                ins.then_inc(k.gives("a_states"), 1)

            def a_att():
                dve.wait_ge(drained("a_g"), k.done("a_g"))
                stt(gr, gth, 1.0, rden, ALU.add, ALU.mult)
                dve.wait_ge(S("a_ylag"), k.at("a_ylag", LAGS - 1))
                dve.wait_ge(filled("a_y"), k.done("a_y"))
                tt(ysum, bank_of("a_y")[:, :], ylag, ALU.add).then_inc(drained("a_y"), 1)
                dve.wait_ge(drained("a_y"), k.done("a_y"))
                stt(att, ysum, 0.5, gr, ALU.mult, ALU.mult).then_inc(k.gives("a_att"), 1)

            def a_out(x, last):
                dve.wait_ge(filled("a_o"), k.done("a_o"))
                tt(x[:, :, :], x[:, :, :], chunks(bank_of("a_o")[:, :]), ALU.add).then_inc(drained("a_o"), 1)

            def over_experts(v):
                return v.unsqueeze(2).broadcast_to([P, CH, E])

            def f_xT():
                dve.wait_ge(S("f_xh"), k.at("f_xh", 1))
                tt(fxl[:, :], bank_of("f_xT")[:, :], f32(fxh[:, :]), ALU.subtract).then_inc(drained("f_xT"), 1)

            def f_logits():
                dve.wait_ge(filled("f_l"), k.done("f_l"))
                bias = gbias[:, :].unsqueeze(1).broadcast_to([P, CH, E])
                tt(lg[:, :, :], bank_of("f_l")[:, 0:CH * E].rearrange("p (c e) -> p c e", c=CH), bias, ALU.add).then_inc(drained("f_l"), 1)
                dve.wait_ge(drained("f_l"), k.done("f_l"))
                dve.tensor_reduce(m1[:, :], lg[:, :, :], AX_X, ALU.max).then_inc(k.gives("step_f_dve"), 1)
                dve.wait_ge(S("step_f_dve"), k.now("step_f_dve"))
                tt(lg2[:, :, :], lg[:, :, :], over_experts(m1[:, :]), ALU.subtract).then_inc(k.gives("f_lg2"), 1)

            def f_choose():
                dve.wait_ge(S("f_ex"), k.at("f_ex", 1))
                dve.tensor_reduce(sm[:, :], ex[:, :, :], AX_X, ALU.add).then_inc(k.gives("step_f_dve"), 1)
                dve.wait_ge(S("step_f_dve"), k.now("step_f_dve"))
                dve.reciprocal(rs1[:, :], sm[:, :]).then_inc(k.gives("step_f_dve"), 1)
                dve.wait_ge(S("step_f_dve"), k.now("step_f_dve"))
                tt(pr[:, :, :], ex[:, :, :], over_experts(rs1[:, :]), ALU.mult).then_inc(k.gives("step_f_dve"), 1)
                dve.wait_ge(S("step_f_dve"), k.now("step_f_dve"))
                dve.memset(tick[:, :], 0.0)
                for c in range(CH):
                    ins = dve.max(top8[:, c, :], pr[:, c, :])
                ins.then_inc(k.gives("step_f_dve"), 1)
                dve.wait_ge(S("step_f_dve"), k.now("step_f_dve"))
                second = over_experts(top8[:, :, 1])
                tt(gt[:, :, :], pr[:, :, :], second, ALU.is_gt)
                tt(need[:, :], top8[:, :, 0], top8[:, :, 1], ALU.is_equal)
                tt(eq[:, :, E:], pr[:, :, :], second, ALU.is_equal).then_inc(k.gives("step_f_dve"), 1)
                dve.wait_ge(S("step_f_dve"), k.now("step_f_dve"))
                tt(eq2[:, :, E:], eq[:, :, E:], eq[:, :, E - 1:-1], ALU.add).then_inc(k.gives("step_f_dve"), 1)
                dve.wait_ge(S("step_f_dve"), k.now("step_f_dve"))
                tt(eq4[:, :, E:], eq2[:, :, E:], eq2[:, :, E - 2:-2], ALU.add).then_inc(k.gives("step_f_dve"), 1)
                dve.wait_ge(S("step_f_dve"), k.now("step_f_dve"))
                tt(eq8[:, :, :], eq4[:, :, E:], eq4[:, :, E - 4:-4], ALU.add).then_inc(k.gives("step_f_dve"), 1)
                dve.wait_ge(S("step_f_dve"), k.now("step_f_dve"))
                stt(keep[:, :, :], eq8[:, :, :], 1.0, over_experts(need[:, :]), ALU.subtract, ALU.is_le).then_inc(k.gives("step_f_dve"), 1)
                dve.wait_ge(S("step_f_dve"), k.now("step_f_dve"))
                tt(kept[:, :, :], keep[:, :, :], eq[:, :, E:], ALU.mult).then_inc(k.gives("step_f_dve"), 1)
                dve.wait_ge(S("step_f_dve"), k.now("step_f_dve"))
                tt(both[:, :, :], kept[:, :, :], gt[:, :, :], ALU.add).then_inc(k.gives("step_f_dve"), 1)
                dve.wait_ge(S("step_f_dve"), k.now("step_f_dve"))
                tt(gate[:, :, :], both[:, :, :], pr[:, :, :], ALU.mult).then_inc(k.gives("f_gate"), 1)

            def f_gT():
                dve.wait_ge(S("f_gTh"), k.at("f_gTh", 1))
                tt(gTl[:, :], bank_of("f_gT")[0:E, :], f32(gTh[:, :]), ALU.subtract).then_inc(drained("f_gT"), 1)

            def f_tile(i):
                if i < NT:
                    dve.wait_ge(drained(f"f_gb{i // 2}"), k.done(f"f_gb{i // 2}"))
                    dve.wait_ge(filled(f"f_z{i}"), k.done(f"f_z{i}"))
                    if i >= HBUF:
                        dve.wait_ge(S("f_h_used"), k.at("f_h_used", i - HBUF + 1))
                    stt(hg[i % HBUF], bank_of(f"f_z{i}")[:, :], nb1[:, i:i + 1], gb[i // 2 % 2], ALU.max, ALU.mult)\
                        .then_inc(drained(f"f_z{i}"), 1)
                n = i - 1
                if n % 2 == 0 and n < NT:
                    dve.wait_ge(S("f_hi"), k.at("f_hi", n + 1))
                    tt(hl[:, n % HBUF, :], hg[n % HBUF], f32(hh[:, n % HBUF, :]), ALU.subtract).then_inc(k.gives("f_lo_even"), 1)

            def f_outT(x, last):
                dve.wait_ge(filled("f_oT"), k.done("f_oT"))
                if last:
                    m, n = k.runs["f"]
                    dve.wait_ge(S("xout_free"), k.value(32, 16 * (n - 2) + 1))
                tt((xout if last else x)[:, :, :], x[:, :, :], chunks(bank_of("f_oT")[:, :]), ALU.add).then_inc(drained("f_oT"), 1)

            def b_xT():
                dve.wait_ge(S("b_xh"), k.at("b_xh", 1))
                tt(bxl[:, :], bank_of("b_xT")[:, :], f32(bxh[:, :]), ALU.subtract)
                dve.tensor_reduce(xsum[:, :], chunks(bank_of("b_xT")[:, :]), AX_X, ALU.add).then_inc(drained("b_xT"), 1)

            def b_qk(g):
                if g == 0:
                    dve.wait_ge(drained("b_xT"), k.done("b_xT"))
                    copy(xpre[:, 1:2], xsum[:, 0:1]).then_inc(k.gives("step_b_dve"), 1)
                    dve.wait_ge(S("step_b_dve"), k.now("step_b_dve"))
                    tt(xpre[:, 2:3], xpre[:, 1:2], xsum[:, 1:2], ALU.add).then_inc(k.gives("step_b_dve"), 1)
                    dve.wait_ge(S("step_b_dve"), k.now("step_b_dve"))
                    tt(xpre[:, 3:4], xpre[:, 2:3], xsum[:, 2:3], ALU.add).then_inc(k.gives("b_xpre"), 1)
                dve.wait_ge(S("b_qk_hi"), k.at("b_qk_hi", 2 * g + 1))
                tt(q2[:, g % 2, :], bank_of(f"b_q{g}")[:, :], f32(q1[:, g % 2, :]), ALU.subtract).then_inc(drained(f"b_q{g}"), 1)
                dve.wait_ge(S("b_qk_hi"), k.at("b_qk_hi", 2 * g + 2))
                stt(kk[:, g % 2, :], bank_of(f"b_k{g}")[:, :], half[:, :], f32(ksg[:, :]), ALU.mult, ALU.subtract).then_inc(drained(f"b_k{g}"), 1)

            def b_v(n):
                if n % 2:
                    dve.wait_ge(filled(f"b_v{n}"), k.done(f"b_v{n}"))
                    copy(vv[:, n // 2, 512:1024], bank_of(f"b_v{n}")[:, :]).then_inc(drained(f"b_v{n}"), 1)

            def b_vpre():
                dve.wait_ge(S("b_xpreh"), k.at("b_xpreh", 1))
                tt(xprel[:, :], xpre[:, :], f32(xpreh[:, :]), ALU.subtract).then_inc(k.gives("b_xprel"), 1)

            def b_s(h):
                for j in (0, 1, 2):
                    dve.wait_ge(drained(f"b_s{h}_{j}"), k.done(f"b_s{h}_{j}"))
                d = pflat[h % PBUF][:, 0:CH * (T + P)].rearrange("p (j n) -> p j n", n=T + P)[:, :, 0:P]
                m = causal[:, :].unsqueeze(1).broadcast_to([P, CH, P])
                stt(d, d, 1.0, m, ALU.add, ALU.mult).then_inc(k.gives("b_diag"), 1)

            def b_y(p):
                dve.wait_ge(drained("b_vpre"), k.done("b_vpre"))
                dve.wait_ge(filled(f"b_y{p}"), k.done(f"b_y{p}"))
                v = vpre[:, p, :].unsqueeze(2).broadcast_to([P, CH, P])
                tt(chunks(ysb[:, p, :]), chunks(bank_of(f"b_y{p}")[:, :]), v, ALU.add).then_inc(drained(f"b_y{p}"), 1)

            def b_ss(p):
                dve.wait_ge(filled(f"b_ss{p}"), k.done(f"b_ss{p}"))
                ts(ssv[:, p, :, :].rearrange("p c a -> p (c a)"), bank_of(f"b_ss{p}")[:, 0:2 * CH], 1.0 / DB, 4 * RMS_EPS, ALU.mult, ALU.add)\
                    .then_inc(drained(f"b_ss{p}"), 1)

            def b_rT():
                dve.wait_ge(S("b_rTh"), k.at("b_rTh", 1))
                tt(rTl, bank_of("b_rT")[0:HB, :], f32(rTh), ALU.subtract).then_inc(drained("b_rT"), 1)

            def b_rb(p):
                if p < NPAIR:
                    dve.wait_ge(filled(f"b_rb{p}"), k.done(f"b_rb{p}"))
                    if p >= 2:
                        dve.wait_ge(S("b_yn_used"), k.at("b_yn_used", p - 1))
                    tt(yn[p % 2], ysb[:, p, :], bank_of(f"b_rb{p}")[:, :], ALU.mult).then_inc(drained(f"b_rb{p}"), 1)

            def b_outT(x, last):
                dve.wait_ge(filled("b_outT"), k.done("b_outT"))
                tt(x[:, :, :], x[:, :, :], chunks(bank_of("b_outT")[:, :]), ALU.add).then_inc(drained("b_outT"), 1)

            run(k, dve, {"a_stats": stats("a"), "b_stats": stats("b"), "f_stats": stats("f"), "a_xhat": xhat("a"), "b_xhat": xhat("b"),
                         "f_xhat": xhat("f"), "a_mix": a_mix, "a_scale": a_scale, "a_products": a_products, "a_lags": a_lags,
                         "a_kends": a_kends, "a_level": a_level, "a_state": a_state, "a_att": a_att, "a_out": a_out,
                         "f_xT": f_xT, "f_logits": f_logits, "f_choose": f_choose, "f_gT": f_gT, "f_tile": f_tile, "f_outT": f_outT,
                         "b_xT": b_xT, "b_qk": b_qk, "b_v": b_v, "b_vpre": b_vpre, "b_s": b_s, "b_y": b_y, "b_ss": b_ss, "b_rT": b_rT,
                         "b_rb": b_rb, "b_outT": b_outT})




def _laid_out(inputs):
    import numpy as np

    i = {n: np.asarray(v) for n, v in inputs.items()}
    a = {"x": i["L0_attn_a_x"], "time_decay": i["L0_attn_a_time_decay"], "norm_scale": i["L0_attn_a_norm_scale"]}
    for n in "qkvgo":
        a[f"WaT_{n}"] = i[f"L0_attn_a_W{n}"].T
    for n in "qkvg":
        a[f"mix_{n}"] = i[f"L0_attn_a_mix_{n}"]
    a["WbqkT"] = np.stack([i["L0_attn_b_Wq"].T, i["L0_attn_b_Wk"].T], axis=1)
    a["WbvT"] = i["L0_attn_b_Wv"].T
    a["WboT"] = i["L0_attn_b_Wo"].T.reshape(NPAIR, P, C).transpose(1, 0, 2)
    a["g_weight"] = i["L0_attn_b_g_weight"]
    a["gate_wT"], a["gate_b"] = i["L0_ffn_gate_w"].T, i["L0_ffn_gate_b"]
    a["w1L"] = i["L0_ffn_w1"].transpose(1, 0, 2).reshape(C, NT, P)
    a["w2L"] = i["L0_ffn_w2"].reshape(NT, P, C).transpose(1, 0, 2)
    a["b1T"] = i["L0_ffn_b1"].reshape(NT, P).T
    a["b2"] = i["L0_ffn_b2"]
    return {n: np.ascontiguousarray(v) for n, v in a.items()}


def kernel(**inputs):
    import concourse.bacc as _bacc
    from concourse.bass_utils import run_bass_kernel_spmd as _run

    arrays = _laid_out(inputs)
    nc = _bacc.Bacc("TRN2", target_bir_lowering=False, num_devices=1)
    args = {n: nc.dram_tensor(f"in_{n}", v.shape, mybir.dt.from_np(v.dtype), kind="ExternalInput").ap() for n, v in arrays.items()}
    out = nc.dram_tensor("result", (B, T, C), F32, kind="ExternalOutput").ap()
    hybrid_block_kernel(nc, args, out)
    return _run(nc, [{f"in_{n}": v for n, v in arrays.items()}], core_ids=[0]).results[0]["result"]
```

```python
from contextlib import ExitStack

import concourse.bass as bass
from concourse import mybir

F32 = mybir.dt.float32
F32R = mybir.dt.float32r
U8 = mybir.dt.uint8
ALU = mybir.AluOpType
ACT = mybir.ActivationFunctionType
AX_X = mybir.AxisListType.X

P = 128
B, T, C = 4, 512, 128
CH = T // P
HA, DA = 4, 32
HB, FB, DB = 16, 16, 64
GB = 4
NPAIR = HB // 2
EARLY = 6
PBUF = 4
E, HID = 8, 256
NT = E * HID // P
HBUF = 3
OUT_LAG = 3
LO_DVE = 2
LAGS = 4
LEVELS = range(2, 7)
LN_EPS, Q_EPS, RMS_EPS = 1e-5, 1e-8, 1e-5
LAG_AT = [0, 512, 896, 1152, 1280]

STEPS_M, STEPS_N = ["m_stats", "m_xhat", "m_xT"], ["n_stats", "n_xhat", "n_xT"]
STEPS_A = ["a_mix", "a_proj", "a_norm", "a_scale", "a_qkT", "a_products", "a_z", "a_lags",
           "a_q0", "a_den", "a_q1", "a_kends", "a_rden", "a_level0", "a_level1", "a_state", "a_level2", "a_level3", "a_level4", "a_y", "a_att", "a_out"]
STEPS_F = ["f_stats", "f_xhat", "f_xT", "f_logits", "f_lT", "f_softmax", "f_choose", "f_gT"]
STEPS_F += [f"f_tile{i}" for i in range(NT + OUT_LAG)] + ["f_out", "f_outT"]
STEPS_B = ["b_qk0"] + [f"b_v{n}" for n in range(4)] + ["b_xp"] + [f"b_v{n}" for n in range(4, 2 * CH)]
STEPS_B += ["b_xl", "b_s0", "b_vp0", "b_s1", "b_qk1", "b_vp1", "b_s2", "b_vp2", "b_s3", "b_vp3"]
STEPS_B += ["b_vpre", "b_av0", "b_y0"]
for _p in range(2, NPAIR):
    STEPS_B += [f"b_s{2 * _p}", f"b_s{2 * _p + 1}"] + ([f"b_qk{_p // 2 + 1}"] if _p in (2, 4) else [])
    STEPS_B += [f"b_av{_p - 1}", f"b_y{_p - 1}", f"b_ss{_p - 2}"]
STEPS_B += ["b_av7", "b_rT0", "b_y7", "b_rb0", "b_ss6", "b_rb1", "b_wo0", "b_ss7", "b_rb2", "b_rb3", "b_rb4", "b_wo1", "b_rb5", "b_wo2"]
STEPS_B += ["b_rT1", "b_wo3", "b_wo4", "b_rb6", "b_rb7", "b_wo5", "b_wo6", "b_wo7", "b_out", "b_outT"]

SHARE = {
    "a_att": 2, "a_den": 0.77, "a_kends": 0.5, "a_lags": 2.12, "a_level": 2.34, "a_mix": 2, "a_norm": 1, "a_out": 1.5,
    "a_products": 2, "a_proj": 4, "a_q": 0.42, "a_qkT": 3.0, "a_rden": 1, "a_scale": 1.5, "a_state": 1.5, "a_y": 2.1,
    "a_z": 1.5, "b_av": 2.2, "b_out": 0.5, "b_outT": 1.5, "b_qk": 1.3, "b_rT": 1, "b_rb": 0.5, "b_s": 1.1,
    "b_ss": 0.9, "b_v": 0.7, "b_vp": 0.8, "b_vpre": 0.5, "b_wo": 0.9, "f_choose": 3, "f_gT": 1.5, "f_lT": 1.5,
    "f_logits": 0.7, "f_out": 1, "f_outT": 3.0, "f_softmax": 1, "f_stats": 2.4, "f_tile": 1.6, "f_xT": 1,
    "f_xhat": 1.5, "m_stats": 2, "m_xT": 1.5, "m_xhat": 0.7, "n_stats": 2, "n_xT": 1.5, "n_xhat": 1,
}


def placed(steps, x, start, end):
    shares = [SHARE.get(s.rstrip("0123456789"), 0.5) for s in steps]
    total, at, out = sum(shares), 0.0, []
    for s, n in zip(steps, shares):
        out.append((start + (at + n / 2) * (end - start) / total, s, x))
        at += n
    return out


def merged(*phases):
    return [(s, x) for _, s, x in sorted(sum(phases, []), key=lambda e: e[0])]


def bank_uses():
    a = [("a_q", 1), ("a_k", 2), ("a_v", 3), ("a_vT", 0), ("a_g", 1), ("a_qT", 2), ("a_kT", 3),
         ("a_r0", 0), ("a_r1", 1), ("a_r23", 2), ("a_den", 3), ("a_ks", 0)]
    for i in range(len(LEVELS)):
        a += [(f"a_s{i}_{u}", 2 * (i % 2) + u) for u in range(2)]
        a += [("a_u", 2)] if i == 1 else []
    a += [("a_y", 2), ("a_o", 3)]
    f = [("f_xT", 6), ("f_l", 6), ("f_lT", 6), ("f_gT", 6)]
    for i in range(NT):
        f += [(f"f_gb{i // 2}", 6)] if i % 2 == 0 else []
        f += [(f"f_z{i}", 4 + i % 2)]
    f += [("f_o", 7), ("f_oT", 6)]
    m, n_ = [("m_xT", 6)], [("n_xT", 6)]
    b, ring = [], 0
    for s in STEPS_B:
        n = s[3:] if s[:3] == "b_s" and s[3:].isdigit() else None
        if n:
            new = [f"b_s{n}_{i}" for i in range(3)]
        elif s[:4] == "b_qk":
            new = [f"b_q{s[4:]}", f"b_k{s[4:]}"]
        elif s[:4] == "b_av":
            b.append((f"b_y{s[4:]}", 0))
            continue
        elif s == "b_vpre":
            b.append((s, 0))
            continue
        elif s == "b_wo0":
            b.append(("b_o", 0))
            continue
        elif s[:4] in ("b_ss", "b_rb", "b_rT") or (s[:3] == "b_v" and s[3:].isdigit()) or s == "b_outT":
            new = [s]
        else:
            continue
        for u in new:
            b.append((u, 1 + ring % 3))
            ring += 1
    place, count = {}, {}
    for phase in (a, f, b, m, n_):
        n = [0] * 8
        for use, bank in phase:
            place[use] = (bank, n[bank])
            n[bank] += 1
        count[phase[0][0][0]] = n
    return place, count


BANK_USES, BANK_COUNT = bank_uses()

STEPS_S = ["s_mask", "s_pow", "s_w0", "s_lo0", "s_w1", "s_lo1", "s_w2", "s_lo2", "s_c", "s_cT", "s_w3", "s_lo3", "s_end"]

PLACES = {
    "first": ((-0.2, 0.0), (0.015, 1.0), (0.03, 0.9), (0.9, 1.0)),
    "a1_f0": ((-0.015, 1.0), (0.05, 0.895), (0.9, 1.0)),
    "b0_f1": ((0.0, 1.0), (0.05, 0.88), (0.9, 1.0)),
    "b1_g0": ((0.0, 1.0), (0.02, 0.85)),
    "a0_g1": ((-0.2, 0.015), (0.045, 1.0), (0.08, 0.88), (0.9, 1.0)),
    "g1": ((0.0, 1.0),),
}
PHASES = {"first": ((STEPS_M, 0), (STEPS_A, 0), (STEPS_S, 0), (STEPS_M, 1)), "a1_f0": ((STEPS_A, 1), (STEPS_F, 0), (STEPS_N, 0)),
          "b0_f1": ((STEPS_B, 0), (STEPS_F, 1), (STEPS_N, 1)), "b1_g0": ((STEPS_B, 1), (STEPS_F, 0)),
          "a0_g1": ((STEPS_M, 0), (STEPS_A, 0), (STEPS_F, 1), (STEPS_M, 1)), "g1": ((STEPS_F, 1),)}
ORDER = {slot: [placed(*phase, *place) for phase, place in zip(PHASES[slot], PLACES[slot])] for slot in PHASES}

FREE_AT_1 = 4

PER = {
    "a_att": 1, "a_klev": 5, "a_kst": 1, "a_lagp": 4, "a_nrm": 1, "a_pmat": 1, "a_qlev": 2, "a_qlev_pool": 3,
    "a_qst": 1, "a_qz": 1, "a_ssq": 8, "a_states": 2, "a_xm": 4, "a_ylag": 3, "b_diag": 16, "b_j2": 16, "b_qk_hi": 8,
    "b_rTh": 2, "b_rr": 8, "b_xpre": 1, "b_xpreh": 1, "b_xprel": 1, "b_ysq": 8, "f_ex": 1, "f_gTh": 1, "f_gate": 1,
    "f_h_used": 16, "f_hi": 16, "f_lg2": 1, "f_lo_dve": 8, "f_lo_pool": 8, "f_mv": 1, "f_rstd": 1, "f_xh": 1,
    "f_xhat": 1, "m_mv": 1, "m_rstd": 1, "m_xhat": 1, "n_mv": 1, "n_rstd": 1, "n_xh": 1, "n_xhat": 1, "step_a_dve": 4,
    "step_a_pool": 1, "step_b_dve": 2, "step_f_dve": 13, "step_f_pool": 1, "step_m_dve": 1, "step_m_pool": 1,
    "step_n_dve": 1, "step_n_pool": 1,
}


def hybrid_block_kernel(nc: bass.Bass, a, out):
    with ExitStack() as ctx:
        def sb(name, shape, dt=F32):
            return ctx.enter_context(nc.sbuf_tensor(name, shape, dt))

        wa_all = sb("wa_all", [P, 5, C])
        wa = {n: wa_all[:, i, :] for i, n in enumerate("qkvgo")}
        cols = sb("cols", [P, 7 + NT])
        mix = {n: cols[:, i:i + 1] for i, n in enumerate("qkvg")}
        nscale, decay0, gcol, b1c = cols[:, 4:5], cols[:, 5:6], cols[:, 6:7], cols[:, 7:7 + NT]
        decay = sb("decay", [P, 2])
        wpow = sb("wpow", [P, P + 1])
        wrev = sb("wrev", [P, P + 1])
        w1h, w1l = sb("w1h", [P, NT, P], F32R), sb("w1l", [P, NT, P], F32R)
        w2h, w2l = sb("w2h", [P, NT, P], F32R), sb("w2l", [P, NT, P], F32R)
        nb1 = sb("nb1", [P, NT])
        b2r, cT, cb = sb("b2r", [E, C]), sb("cT", [P, E]), sb("cb", [E, C])
        gw, gwh, gwl = sb("gw", [P, E]), sb("gwh", [P, E], F32R), sb("gwl", [P, E], F32R)
        gbias = sb("gbias", [P, E])
        wqkh, wqkl = sb("wqkh", [P, 2 * GB, P], F32R), sb("wqkl", [P, 2 * GB, P], F32R)
        wbvh, wbvl = sb("wbvh", [P, HB * DB], F32R), sb("wbvl", [P, HB * DB], F32R)
        wbo = sb("wbo", [P, NPAIR, C])
        ident, identr = sb("ident", [P, P]), sb("identr", [P, P], F32R)
        hsel = sb("hsel", [2 * EARLY, EARLY, P], F32R)
        causal = sb("causal", [P, P])
        headsum = sb("headsum", [P, P])
        whead = sb("whead", [P, HA, 64])
        pairsel = sb("pairsel", [P, 2])
        half, sgn = sb("half", [P, 1]), sb("sgn", [P, 1])
        lmask = sb("lmask", [P, len(LEVELS), 64], U8)
        mhalf, phalf = sb("mhalf", [P, 8]), sb("phalf", [P, 8])
        lneps, overc = sb("lneps", [P, CH]), sb("overc", [P, 8])
        tick, unread = sb("tick", [P, 1]), sb("unread", [P, 16])

        xs, xout = [sb("x0", [P, CH, C]), sb("x1", [P, CH, C])], sb("xout", [P, CH, C])
        xhat, st6, mv = sb("xhat", [P, CH, C]), sb("st6", [P, CH, 6]), sb("mv", [P, CH, 2])
        ve, rstd = sb("ve", [P, CH]), sb("rstd", [P, CH])
        fxh, fxl = sb("fxh", [P, T], F32R), sb("fxl", [P, T], F32R)
        bxh, bxl = sb("bxh", [P, T], F32R), sb("bxl", [P, T], F32R)

        big = sb("big", [P, 37 * T])
        bigr = sb("bigr", [P, (6 + 2 * HBUF) * T], F32R)

        def cut(at, n=1):
            return big[:, at * T:(at + n) * T]

        def cutr(at, n):
            return bigr[:, at * T:(at + n) * T].rearrange("p (j n) -> p j n", n=T)

        w1in = w2in = cut(31, 4).rearrange("p (i n) -> p i n", i=NT)
        wbvin = cut(35, 2)
        wqkin = cut(30).rearrange("p (a n) -> p a n", a=2)
        lmask_f = cut(29)[:, 0:len(LEVELS) * 64].rearrange("p (i n) -> p i n", n=64)

        xTs = sb("xTs", [P, T + 1])
        xdiff = cut(0)
        xm = {n: cut(1 + i) for i, n in enumerate("qkvg")}
        ssq, ms, nrm, nrme, rn = (sb(n, [P, 8]) for n in ("ssq", "ms", "nrm", "nrme", "rn"))
        qk_n = cut(6, 2).rearrange("p (a c n) -> p a c n", a=2, c=CH)
        qe, ke = cut(8), cut(9)
        vtok = cut(10).rearrange("p (c n) -> p c n", c=CH)
        vch, gth = cut(11), cut(12)
        lagp = cut(13, 3)
        squares = cut(13, 2)
        z, qz, ylag = cut(16), cut(17), cut(18)
        ytmp = cut(19, 3)
        qlev = cut(0, 4).rearrange("p (a n) -> p a n", a=2)
        klev = sb("klev", [P, 2, T])
        qst, kst = cut(23), cut(24)
        kstT = cut(25).rearrange("p (c n) -> p c n", c=CH)
        rden, ysum, gr, att = cut(26), cut(27), cut(28), cut(29)
        pbuf = sb("pbuf", [P, 5 * T])
        pmat = pbuf[:, 0:4 * T].rearrange("p (h c n) -> p h c n", h=HA, c=CH)
        states = sb("states", [P, 3, P])

        lg, ex, pr = sb("lg", [P, CH, E]), sb("ex", [P, CH, E]), sb("pr", [P, CH, E])
        lg2 = sb("lg2", [P, CH, E])
        m1, sm, rs1, need = sb("m1", [P, CH]), sb("sm", [P, CH]), sb("rs1", [P, CH]), sb("need", [P, CH])
        top8 = sb("top8", [P, CH, 8])
        gt, gate = sb("gt", [P, CH, E]), sb("gate", [P, CH, E])
        eq, eq2, eq4 = (sb(n, [P, CH, 2 * E]) for n in ("eq", "eq2", "eq4"))
        eq8, keep, kept = sb("eq8", [P, CH, E]), sb("keep", [P, CH, E]), sb("kept", [P, CH, E])
        both = sb("both", [P, CH, E])
        gb = [cut(30), cut(31)]
        hg = [cut(32 + i) for i in range(HBUF)]
        oT, gT = cut(35), cut(36)[0:E, :]
        hh, hl = cutr(6, HBUF), cutr(6 + HBUF, HBUF)
        gTh, gTl = sb("gTh", [E, T], F32R), sb("gTl", [E, T], F32R)

        q1, q2, kk = cutr(0, 2), cutr(2, 2), cutr(4, 2)
        ksg = sb("ksg", [P, T], F32R)
        pflat = [big[:, 4 * i * T:(4 * i + 5) * T] for i in range(PBUF - 1)] + [pbuf]
        vv = cut(12, 8).rearrange("p (c n) -> p c n", c=CH)
        ysb = cut(20, 8).rearrange("p (q n) -> p q n", q=NPAIR)
        ysq = [cut(28), cut(29)]
        boT = cut(0)
        xsum, xpre = sb("xsum", [P, CH]), sb("xpre", [P, CH])
        xpreh, xprel = sb("xpreh", [P, CH], F32R), sb("xprel", [P, CH], F32R)
        vpre = sb("vpre", [P, NPAIR, CH])
        ssv, rr = sb("ssv", [P, NPAIR, CH, 2]), sb("rr", [P, CH, NPAIR, 2])
        rTh, rTl = bigr[0:2 * EARLY, 0:T], bigr[0:2 * EARLY, T:2 * T]

        bank = [ctx.enter_context(nc.psum_tensor(f"bank{i}", [P, 512], F32)) for i in range(8)]
        sems = {}

        def S(name):
            if name not in sems:
                sems[name] = ctx.enter_context(nc.semaphore("s_" + name))
            return sems[name]

        def bank_of(use):
            return bank[BANK_USES[use][0]]

        def filled(use):
            return S(f"filled{BANK_USES[use][0]}")

        def drained(use):
            return S(f"drained{BANK_USES[use][0]}")

        block = ctx.enter_context(nc.Block())

        class Count:

            def __init__(self):
                self.it, self.runs, self.given = None, {"a": (0, 0), "b": (0, 0), "f": (0, 0), "m": (0, 0), "n": (0, 0)}, {}

            def value(self, m, n):
                return n if self.it is None or m == 0 else self.it * m + n

            def gives(self, name):
                self.given[name] = self.given.get(name, 0) + 1
                return S(name)

            def at(self, name, n):
                per, (m, r) = PER.get(name, 1), self.runs[name[name.startswith("step_") * 5]]
                return self.value(m * per, r * per + n)

            def now(self, name):
                return self.at(name, self.given[name])

            def uses(self, use, n):
                b, k = BANK_USES[use]
                m, r = 0, k + n + (b >= FREE_AT_1)
                for phase in ("ab" if use[0] in "ab" else "fmn"):
                    pm, pr_ = self.runs[phase]
                    m, r = m + pm * BANK_COUNT[phase][b], r + pr_ * BANK_COUNT[phase][b]
                return self.value(m, r)

            def before(self, use):
                return self.uses(use, 0)

            def before_slot(self, use):
                return self.uses(use, -BANK_USES[use][1])

            def done(self, use):
                return self.uses(use, 1)

            def normed(self):
                return self.before_slot("m_xT")

            def end(self, phase):
                for name, n in list(self.given.items()):
                    if name[name.startswith("step_") * 5] == phase:
                        assert PER.get(name, 1) == n, (name, n)
                        del self.given[name]
                m, r = self.runs[phase]
                self.runs[phase] = (m, r + 1)

        def run(k, eng, steps):

            def slot(items, last):
                for name, x in items:
                    kind, n = name.rstrip("0123456789"), name[len(name.rstrip("0123456789")):]
                    if kind in steps:
                        of_x = kind[2:] in ("stats", "xhat", "out", "outT")
                        steps[kind](*([int(n)] if n else []), **({"x": xs[x], "last": last} if of_x else {}))
                    if name in ("a_out", "b_outT", "f_outT", "m_xT", "n_xT"):
                        k.end(name[0])

            k.runs = {"a": (0, 0), "b": (0, 0), "f": (0, 0), "m": (0, 0), "n": (0, 0)}
            slot(merged(*ORDER["first"]), False)
            with eng.Fori(0, B // 2) as it:
                k.it = it
                k.runs = {"a": (2, 1), "b": (2, 0), "f": (4, 0), "m": (2, 2), "n": (2, 0)}
                slot(merged(*ORDER["a1_f0"]), False)
                slot(merged(*ORDER["b0_f1"]), False)
                slot(merged(*ORDER["b1_g0"]), True)
                with eng.If(it < B // 2 - 1):
                    before = dict(k.runs)
                    slot(merged(*ORDER["a0_g1"]), True)
                with eng.Else():
                    k.runs = before
                    slot(merged(*ORDER["g1"]), True)
            k.it = None

        def chunks(ap):
            return ap.rearrange("p (c n) -> p c n", c=CH)

        def cs(c):
            return slice(c * P, (c + 1) * P)

        def gates_at(i):
            return 0 if i == 0 else (i + 1) // 2 if i % 2 and i + 1 < NT else None

        def lo_of(n):
            by_dve = n // LO_DVE + 1
            return ("f_lo_dve", by_dve) if n % LO_DVE == 0 else ("f_lo_pool", n + 1 - by_dve)

        def q_times_w(i):
            n = 2 ** LEVELS[i]
            blocks = T // (2 * n)
            w = whead[:, :, 0:n].unsqueeze(1).broadcast_to([P, blocks, HA, n])
            q = halves(qe, LEVELS[i], True).unsqueeze(2).broadcast_to([P, blocks, HA, n])
            return qlev[:, i % 2, :].rearrange("p (b h n) -> p b h n", h=HA, n=n), q, w

        def pairs_of(i):
            return (EARLY, NPAIR - EARLY)[i]

        def lag_view(ap, first, n):
            return ap.rearrange("p (b l) -> p b l", l=LAGS)[:, :, first:first + n]

        def lag_part(ap, lag, base=0):
            return ap[:, LAG_AT[lag] - base:LAG_AT[lag + 1] - base].rearrange("p (b l) -> p b l", l=LAGS - lag)

        def halves(ap, j, upper):
            return ap.rearrange("p (b u n) -> p b u n", u=2, n=2 ** j)[:, :, int(upper), :]

        def f32(ap):
            return ap.bitcast(F32)

        @block.sync
        def _(sp):
            k = Count()

            def col(ap):
                return ap.rearrange("(p o) -> p o", o=1)

            def rows(ap):
                return ap.rearrange("(c p) n -> p c n", p=P)

            sp.dma_start(xs[0][:, :, :], rows(a["x"][0])).then_inc(S("x_in0"), 16)
            sp.dma_start(cols[:, :], a["cols"]).then_inc(S("cols_in"), 16)
            sp.dma_start(wa_all[:, :, :], a["WaT"]).then_inc(S("wa_in"), 16)
            sp.dma_start(w1in, a["w1L"]).then_inc(S("w1_in"), 16)
            sp.dma_start(xs[1][:, :, :], rows(a["x"][1])).then_inc(S("x_in1"), 16)
            for dst, src in ((b2r[:, :], a["b2"]), (gw[:, :], a["gate_wT"]), (gbias[:, :], a["gate_b"].partition_broadcast(P)),
                             (wqkin, a["WbqkT"]), (wbvin, a["WbvT"]), (wbo[:, :, :], a["WboT"])):
                sp.dma_start(dst, src).then_inc(S("wb_in"), 16)
            sp.wait_ge(S("w1_split"), 1)
            sp.dma_start(w2in, a["w2L"]).then_inc(S("w2_in"), 16)
            for row in range(B):
                k.runs.update(f=(0, 4 * (row // 2) + 2 + row % 2), m=(0, (2, 3, 4, 4)[row]), n=(0, 2 * (row // 2) + 2))
                sp.wait_ge(drained("f_oT"), k.done("f_oT"))
                sp.dma_start(rows(out[row]), xout[:, :, :]).then_inc(S("xout_free"), 16)
                if row + 2 < B:
                    sp.dma_start(xs[row % 2][:, :, :], rows(a["x"][row + 2])).then_inc(S(f"x_in{row % 2}"), 16)
            sp.wait_ge(S("xout_free"), 16 * B + 1)

        WB_IN = 16 * 6

        @block.gpsimd
        def _(pool):
            k = Count()
            pool.memset(ident[:, :], 0.0).then_inc(S("pool_setup"), 1)
            pool.wait_ge(S("pool_setup"), 1)
            pool.affine_select(out=ident[:, :], in_=ident[:, :], compare_op=ALU.not_equal, fill=1.0, base=0,
                               pattern=[[-1, P]], channel_multiplier=1).then_inc(S("ident"), 1)
            for t, v in ((mhalf, -0.5), (phalf, 0.5), (lneps, LN_EPS), (overc, 1.0 / C)):
                pool.memset(t[:, :], v).then_inc(S("filled_once"), 1)
            pool.memset(klev[:, :, :], 0.0).then_inc(S("filled_once"), 1)
            pool.wait_ge(S("filled_once"), 5)

            def s_mask():
                pool.memset(lmask_f, 1.0).then_inc(S("pool_setup"), 1)
                for i, j in enumerate(LEVELS):
                    m = lmask_f[:, i, :].rearrange("p (b n) -> p b n", n=2 ** j)
                    size = 2 ** (j + 1)
                    pool.wait_ge(S("pool_setup"), 2 * i + 2)
                    pool.affine_select(out=m, in_=m, compare_op=ALU.is_ge, fill=0.0, base=0,
                                       pattern=[[-size, P // size], [0, 2 ** j]], channel_multiplier=1).then_inc(S("pool_setup"), 1)
                    pool.wait_ge(S("pool_setup"), 2 * i + 3)
                    pool.affine_select(out=m, in_=m, compare_op=ALU.is_ge, fill=0.0, base=2 ** j - 1,
                                       pattern=[[size, P // size], [0, 2 ** j]], channel_multiplier=-1).then_inc(S("pool_setup"), 1)
                pool.memset(causal[:, :], 1.0).then_inc(S("pool_setup"), 1)
                pool.wait_ge(S("pool_setup"), 2 * len(LEVELS) + 3)
                pool.affine_select(out=causal[:, :], in_=causal[:, :], compare_op=ALU.is_ge, fill=0.0, base=0,
                                   pattern=[[1, P]], channel_multiplier=-1).then_inc(S("causal"), 1)

            def stats(ph):
                def step(x, last):
                    pool.wait_ge(S(f"{ph}_mv"), k.at(f"{ph}_mv", 1))
                    pool.tensor_tensor(ve[:, :], mv[:, :, 1], lneps[:, :], ALU.add).then_inc(k.gives(f"step_{ph}_pool"), 1)
                    pool.wait_ge(S(f"step_{ph}_pool"), k.now(f"step_{ph}_pool"))
                    pool.tensor_tensor(rstd[:, :], ve[:, :], mhalf[:, 0:CH], ALU.pow).then_inc(k.gives(f"{ph}_rstd"), 1)
                return step

            def a_mix():
                if k.it is not None:
                    for use in ("a_y", f"b_y{NPAIR - 1}"):
                        pool.wait_ge(filled(use), k.before_slot(use))
                    pool.tensor_tensor(unread[:, 8:9], mhalf[:, 0:1], mhalf[:, 0:1], ALU.add)
                pool.memset(pmat, 0.0).then_inc(k.gives("a_pmat"), 1)

            def a_norm():
                pool.wait_ge(S("a_ssq"), k.at("a_ssq", 8))
                pool.tensor_tensor(ms[:, :], ssq[:, :], overc[:, :], ALU.mult).then_inc(k.gives("step_a_pool"), 1)
                pool.wait_ge(S("step_a_pool"), k.now("step_a_pool"))
                pool.tensor_tensor(nrm[:, :], ms[:, :], phalf[:, :], ALU.pow).then_inc(k.gives("a_nrm"), 1)

            def a_klev(i):
                n = 2 ** LEVELS[i]
                if i >= 2:
                    pool.wait_ge(filled(f"a_s{i - 2}_1"), k.done(f"a_s{i - 2}_1"))
                w = wrev[:, P - n:P].unsqueeze(1).broadcast_to([P, T // (2 * n), n])
                pool.tensor_tensor(halves(klev[:, i % 2, :], LEVELS[i], False), halves(ke, LEVELS[i], False), w, ALU.mult)\
                    .then_inc(k.gives("a_klev"), 1)

            def a_products():
                pool.wait_ge(drained("a_kT"), k.done("a_kT"))
                w = wrev[:, 1:P + 1].unsqueeze(1).broadcast_to([P, CH - 1, P])
                pool.tensor_tensor(chunks(kst)[:, 0:3, :], chunks(ke)[:, 0:3, :], w, ALU.mult).then_inc(k.gives("a_kst"), 1)
                a_klev(0)
                a_klev(1)

            def a_kends():
                w = wpow[:, 1:P + 1].unsqueeze(1).broadcast_to([P, CH - 1, P])
                pool.tensor_tensor(chunks(qst)[:, 1:, :], chunks(qe)[:, 1:, :], w, ALU.mult).then_inc(k.gives("a_qst"), 1)

            def a_level(i):
                if i >= 1 and i + 1 < len(LEVELS):
                    a_klev(i + 1)
                    pool.tensor_tensor(*q_times_w(i + 1), ALU.mult).then_inc(k.gives("a_qlev_pool"), 1)

            def a_state():
                pool.wait_ge(drained("a_r0"), k.done("a_r0"))
                for lag in range(1, LAGS):
                    use = "a_r1" if lag == 1 else "a_r23"
                    pool.wait_ge(drained(use), k.done(use))
                    y = lag_view(ylag, lag, LAGS - lag)
                    pool.tensor_tensor(y, y, lag_part(ytmp, lag, T), ALU.add).then_inc(k.gives("a_ylag"), 1)
                    if lag < LAGS - 1:
                        pool.wait_ge(S("a_ylag"), k.at("a_ylag", lag))

            def f_tile(i):
                n = i - 1
                if 0 <= n < NT and n % LO_DVE:
                    pool.wait_ge(S("f_hi"), k.at("f_hi", n + 1))
                    if n >= HBUF:
                        pool.wait_ge(S("f_h_used"), k.at("f_h_used", n - HBUF + 1))
                    pool.tensor_tensor(hl[:, n % HBUF, :], hg[n % HBUF], f32(hh[:, n % HBUF, :]), ALU.subtract)\
                        .then_inc(k.gives("f_lo_pool"), 1)

            def b_ss(p):
                pool.wait_ge(drained(f"b_ss{p}"), k.done(f"b_ss{p}"))
                pool.tensor_tensor(rr[:, :, p, :], ssv[:, p, :, :], mhalf[:, :].rearrange("p (c a) -> p c a", a=2), ALU.pow)\
                    .then_inc(k.gives("b_rr"), 1)

            run(k, pool, {"s_mask": s_mask, "m_stats": stats("m"), "n_stats": stats("n"), "f_stats": stats("f"), "a_mix": a_mix, "a_norm": a_norm,
                          "a_products": a_products, "a_kends": a_kends, "a_level": a_level, "a_state": a_state, "f_tile": f_tile, "b_ss": b_ss})

        @block.scalar
        def _(act):
            k = Count()
            act.wait_ge(S("cols_in"), 16)
            act.activation(decay[:, 0:1], decay0, ACT.Exp).then_inc(S("exp_decay"), 1)
            act.wait_ge(S("exp_decay"), 1)
            act.activation(decay[:, 1:2], decay[:, 0:1], ACT.Exp, scale=-1.0).then_inc(S("w"), 1)

            def s_w(i):
                if i == 0:
                    act.wait_ge(S("w1_in"), 16)
                    act.activation(w1h[:, :, :], w1in, ACT.Copy).then_inc(S("w_hi"), 1)
                elif i == 3:
                    act.wait_ge(S("w2_in"), 16)
                    act.activation(w2h[:, :, :], w2in, ACT.Copy).then_inc(S("w_hi"), 1)
                elif i == 1:
                    act.wait_ge(S("wb_in"), WB_IN)
                    act.activation(wbvh[:, :], wbvin, ACT.Copy).then_inc(S("w_hi"), 1)
                else:
                    act.activation(gwh[:, :], gw[:, :], ACT.Copy).then_inc(S("w_hi"), 1)
                    dst = wqkh[:, :, :].rearrange("p g (h u f) -> p (g h) u f", u=2, f=FB)
                    src = wqkin.rearrange("p a (h f) -> p (a h) f", f=FB)
                    for u in range(2):
                        act.activation(dst[:, :, u, :], src, ACT.Copy).then_inc(S("w_hi"), 1)

            def s_c():
                act.wait_ge(S("cT_full"), 1)
                act.activation(cT[:, :], bank[4][:, 0:E], ACT.Copy).then_inc(S("cT"), 1)

            def m_xT():
                act.wait_ge(filled("m_xT"), k.done("m_xT"))
                act.activation(xTs[:, 1:T + 1], bank_of("m_xT")[:, :], ACT.Copy).then_inc(drained("m_xT"), 1)

            def a_proj():
                for i, n in enumerate("qk"):
                    act.wait_ge(filled(f"a_{n}"), k.done(f"a_{n}"))
                    for c in range(CH):
                        act.activation(squares[:, (i * CH + c) * P:(i * CH + c + 1) * P], bank_of(f"a_{n}")[:, cs(c)], ACT.Square,
                                       accum_out=ssq[:, i * CH + c:i * CH + c + 1]).then_inc(k.gives("a_ssq"), 1)
                act.wait_ge(filled("a_v"), k.done("a_v"))
                act.activation(vtok.rearrange("p c n -> p (c n)"), bank_of("a_v")[:, :], ACT.Copy).then_inc(drained("a_v"), 1)
                act.wait_ge(filled("a_vT"), k.done("a_vT"))
                act.activation(vch, bank_of("a_vT")[:, :], ACT.Copy).then_inc(drained("a_vT"), 1)

            def a_qkT():
                act.wait_ge(filled("a_qT"), k.done("a_qT"))
                act.activation(qe, bank_of("a_qT")[:, :], ACT.Exp, scale=nscale).then_inc(drained("a_qT"), 1)
                act.wait_ge(filled("a_kT"), k.done("a_kT"))
                act.activation(ke, bank_of("a_kT")[:, :], ACT.Exp, scale=nscale).then_inc(drained("a_kT"), 1)
                act.wait_ge(filled("a_g"), k.done("a_g"))
                act.activation(gth, bank_of("a_g")[:, :], ACT.Tanh, scale=0.5).then_inc(drained("a_g"), 1)

            def a_kends():
                act.wait_ge(filled("a_ks"), k.done("a_ks"))
                act.activation(kstT[:, 0:3, :].rearrange("p c n -> p (c n)"), bank_of("a_ks")[:, 0:3 * P], ACT.Copy)\
                    .then_inc(drained("a_ks"), 1)

            def hi_of_x(use, dst, name):
                act.wait_ge(filled(use), k.done(use))
                act.activation(dst[:, :], bank_of(use)[:, :], ACT.Copy).then_inc(k.gives(name), 1)

            def f_logits():
                act.wait_ge(filled("f_l"), k.done("f_l"))
                act.activation(gT, bank_of("f_l")[0:E, :], ACT.Copy).then_inc(drained("f_l"), 1)

            def f_softmax():
                act.wait_ge(S("f_lg2"), k.at("f_lg2", 1))
                act.activation(ex[:, :, :], lg2[:, :, :], ACT.Exp).then_inc(k.gives("f_ex"), 1)

            def f_gT():
                act.wait_ge(filled("f_gT"), k.done("f_gT"))
                act.activation(gT, bank_of("f_gT")[0:E, :], ACT.Copy)
                act.activation(gTh[:, :], bank_of("f_gT")[0:E, :], ACT.Copy).then_inc(k.gives("f_gTh"), 1)

            def f_tile(i):
                e = gates_at(i)
                if e is not None:
                    act.wait_ge(filled(f"f_gb{e}"), k.done(f"f_gb{e}"))
                    if e >= 2:
                        act.wait_ge(drained(f"f_z{2 * e - 3}"), k.done(f"f_z{2 * e - 3}"))
                    act.activation(gb[e % 2], bank_of(f"f_gb{e}")[:, :], ACT.Copy).then_inc(drained(f"f_gb{e}"), 1)
                n = i - 1
                if 0 <= n < NT:
                    act.wait_ge(drained(f"f_z{n}"), k.done(f"f_z{n}"))
                    if n >= HBUF:
                        act.wait_ge(S("f_h_used"), k.at("f_h_used", n - HBUF + 1))
                    act.activation(hh[:, n % HBUF, :], hg[n % HBUF], ACT.Copy).then_inc(k.gives("f_hi"), 1)

            def f_out(x, last):
                act.wait_ge(filled("f_o"), k.done("f_o"))
                act.activation(oT, bank_of("f_o")[:, :], ACT.Copy).then_inc(drained("f_o"), 1)

            def b_qk(g):
                if g >= 2:
                    use = f"b_s{4 * g - 5}_2"
                    act.wait_ge(filled(use), k.done(use))
                act.wait_ge(filled(f"b_q{g}"), k.done(f"b_q{g}"))
                act.activation(q1[:, g % 2, :], bank_of(f"b_q{g}")[:, :], ACT.Copy).then_inc(k.gives("b_qk_hi"), 1)
                act.wait_ge(filled(f"b_k{g}"), k.done(f"b_k{g}"))
                if g >= 1:
                    act.wait_ge(drained(f"b_k{g - 1}"), k.done(f"b_k{g - 1}"))
                act.activation(ksg[:, :], bank_of(f"b_k{g}")[:, :], ACT.Copy, scale=sgn[:, :]).then_inc(k.gives("b_qk_hi"), 1)

            def b_v(n):
                if n % 2 == 0:
                    act.wait_ge(filled(f"b_v{n}"), k.done(f"b_v{n}"))
                    act.activation(vv[:, n // 2, 0:512], bank_of(f"b_v{n}")[:, :], ACT.Copy).then_inc(drained(f"b_v{n}"), 1)

            def b_xp():
                act.wait_ge(S("b_xpre"), k.at("b_xpre", 1))
                act.activation(xpreh[:, :], xpre[:, :], ACT.Copy).then_inc(k.gives("b_xpreh"), 1)

            def b_vpre():
                act.wait_ge(filled("b_vpre"), k.done("b_vpre"))
                act.activation(vpre[:, :, :].rearrange("p q c -> p (q c)"), bank_of("b_vpre")[:, 0:NPAIR * CH], ACT.Copy)\
                    .then_inc(drained("b_vpre"), 1)

            def b_s(h):
                if h >= PBUF:
                    use = f"b_y{(h - PBUF) // 2}"
                    act.wait_ge(filled(use), k.done(use))
                for j in range(CH):
                    use = f"b_s{h}_{min(j, 2)}"
                    if j < 3:
                        act.wait_ge(filled(use), k.done(use))
                    at = 2 * P if j == 3 else 0
                    act.activation(pflat[h % PBUF][:, j * (T + P):(j + 1) * T], bank_of(use)[:, at:at + T - j * P], ACT.Square,
                                   bias=1.0, scale=0.25).then_inc(k.gives("b_j2") if j == 2 else drained(use), 1)

            def b_y(p):
                act.wait_ge(drained(f"b_y{p}"), k.done(f"b_y{p}"))
                if p >= 2:
                    act.wait_ge(filled(f"b_ss{p - 2}"), k.done(f"b_ss{p - 2}"))
                act.activation(ysq[p % 2], ysb[:, p, :], ACT.Square).then_inc(k.gives("b_ysq"), 1)

            def b_rT(i):
                n = 2 * pairs_of(i)
                act.wait_ge(filled(f"b_rT{i}"), k.done(f"b_rT{i}"))
                act.activation(rTh[0:n, :], bank_of(f"b_rT{i}")[0:n, :], ACT.Copy).then_inc(k.gives("b_rTh"), 1)

            def b_out(x, last):
                act.wait_ge(filled("b_o"), k.done("b_o"))
                act.activation(boT, bank_of("b_o")[:, :], ACT.Copy).then_inc(drained("b_o"), 1)

            run(k, act, {"s_w": s_w, "s_c": s_c, "m_xT": m_xT, "a_proj": a_proj, "a_qkT": a_qkT, "a_kends": a_kends,
                         "f_xT": lambda: hi_of_x("f_xT", fxh, "f_xh"), "f_logits": f_logits, "f_softmax": f_softmax, "f_gT": f_gT, "f_tile": f_tile, "f_out": f_out,
                         "n_xT": lambda: hi_of_x("n_xT", bxh, "n_xh"), "b_qk": b_qk, "b_v": b_v, "b_xp": b_xp, "b_vpre": b_vpre, "b_s": b_s, "b_y": b_y,
                         "b_rT": b_rT, "b_out": b_out})

        @block.tensor
        def _(pe):
            k = Count()
            mm = pe.matmul
            pe.wait_ge(S("ident"), 1)

            def s_c():
                pe.wait_ge(S("w2_in"), 16)
                for i in range(NT):
                    ins = mm(bank[4][:, i // 2:i // 2 + 1], w2in[:, i, :], b1c[:, i:i + 1], start=(i % 2 == 0), stop=(i % 2 == 1))
                ins.then_inc(S("cT_full"), 1)

            def s_cT():
                pe.wait_ge(S("cT"), 1)
                pe.transpose(bank[5][0:E, 0:C], cT[:, :], ident[:, :]).then_inc(S("cb_full"), 1)

            def s_end():
                pe.wait_ge(S("setup_done"), 1)

            def transposes(use, src, n=P, count=CH):
                pe.wait_ge(drained(use), k.before(use))
                for c in range(count):
                    ins = pe.transpose(bank_of(use)[0:n, cs(c)], src(c), ident[:, :])
                ins.then_inc(filled(use), 1)

            def three(o, lhs, rhs, start=True, stop=True):
                mm(o, lhs[0], rhs[0], start=start, stop=False)
                mm(o, lhs[0], rhs[1], start=False, stop=False)
                return mm(o, lhs[1], rhs[0], start=False, stop=stop)

            def m_xT():
                pe.wait_ge(S("m_xhat"), k.at("m_xhat", 1))
                transposes("m_xT", lambda c: xhat[:, c, :])

            def a_proj():
                if k.it is None:
                    pe.wait_ge(S("wa_in"), 16)
                for i, n in enumerate("qkv"):
                    pe.wait_ge(S("a_xm"), k.at("a_xm", i + 1))
                    pe.wait_ge(drained(f"a_{n}"), k.before(f"a_{n}"))
                    for c in range(CH):
                        ins = mm(bank_of(f"a_{n}")[:, cs(c)], xm[n][:, cs(c)], wa[n], start=True, stop=True)
                    ins.then_inc(filled(f"a_{n}"), 1)
                pe.wait_ge(drained("a_vT"), k.before("a_vT"))
                mm(bank_of("a_vT")[:, :], wa["v"], xm["v"], start=True, stop=True).then_inc(filled("a_vT"), 1)

            def a_scale():
                pe.wait_ge(S("a_xm"), k.at("a_xm", 4))
                pe.wait_ge(drained("a_g"), k.before("a_g"))
                mm(bank_of("a_g")[:, :], wa["g"], xm["g"], start=True, stop=True).then_inc(filled("a_g"), 1)

            def a_qkT():
                for i, n in enumerate("qk"):
                    pe.wait_ge(drained(f"a_{n}"), k.done(f"a_{n}"))
                    transposes(f"a_{n}T", lambda c: qk_n[:, i, c, :])

            def a_lags():
                for lag, use in enumerate(("a_r0", "a_r1", "a_r23", "a_r23")):
                    pe.wait_ge(S("a_lagp"), k.at("a_lagp", lag + 1))
                    if lag < 3:
                        pe.wait_ge(drained(use), k.before(use))
                    at, n = (256 if lag == 3 else 0), LAG_AT[lag + 1] - LAG_AT[lag]
                    ins = mm(bank_of(use)[:, at:at + n], headsum[:, :], lagp[:, LAG_AT[lag]:LAG_AT[lag + 1]], start=True, stop=True)
                    if lag != 2:
                        ins.then_inc(filled(use), 1)

            def a_den():
                pe.wait_ge(S("a_qz"), k.at("a_qz", 1))
                pe.wait_ge(drained("a_den"), k.before("a_den"))
                mm(bank_of("a_den")[:, :], headsum[:, :], qz, start=True, stop=True).then_inc(filled("a_den"), 1)

            def a_kends():
                pe.wait_ge(S("a_kst"), k.at("a_kst", 1))
                transposes("a_ks", lambda c: kst[:, cs(c)], count=3)

            def a_level(i):
                pe.wait_ge(S("a_klev"), k.at("a_klev", i + 1))
                q = "a_qlev" if i < 2 else "a_qlev_pool"
                pe.wait_ge(S(q), k.at(q, i + 1 if i < 2 else i - 1))
                for c in range(CH):
                    use = f"a_s{i}_{c // 2}"
                    if c % 2 == 0:
                        pe.wait_ge(drained(use), k.before(use))
                    ins = mm(bank_of(use)[:, c % 2 * 256:(c % 2 + 1) * 256], klev[:, i % 2, cs(c)], qlev[:, i % 2, c * 256:(c + 1) * 256],
                             start=True, stop=True)
                    if c % 2:
                        ins.then_inc(filled(use), 1)

            def a_state():
                pe.wait_ge(drained("a_ks"), k.done("a_ks"))
                pe.wait_ge(drained("a_u"), k.before("a_u"))
                for c in range(3):
                    ins = mm(bank_of("a_u")[:, cs(c)], kstT[:, c, :], vtok[:, c, :], start=True, stop=True)
                ins.then_inc(filled("a_u"), 1)

            def a_y():
                pe.wait_ge(S("a_states"), k.at("a_states", 2))
                pe.wait_ge(S("a_qst"), k.at("a_qst", 1))
                pe.wait_ge(drained("a_s4_1"), k.done("a_s4_1"))
                pe.wait_ge(drained("a_y"), k.before("a_y"))
                for c in range(CH):
                    if c:
                        mm(bank_of("a_y")[:, cs(c)], states[:, c - 1, :], qst[:, cs(c)], start=True, stop=False)
                    for h in range(HA):
                        r = slice(32 * h, 32 * h + 32)
                        ins = mm(bank_of("a_y")[r, cs(c)], vtok[:, c, r], pmat[:, h, c, :], start=(c == 0), stop=True)
                ins.then_inc(filled("a_y"), 1)

            def a_out(x, last):
                pe.wait_ge(S("a_att"), k.at("a_att", 1))
                pe.wait_ge(drained("a_o"), k.before("a_o"))
                for c in range(CH):
                    ins = mm(bank_of("a_o")[:, cs(c)], att[:, cs(c)], wa["o"], start=True, stop=True)
                ins.then_inc(filled("a_o"), 1)

            def f_xT():
                pe.wait_ge(S("f_xhat"), k.at("f_xhat", 1))
                transposes("f_xT", lambda c: xhat[:, c, :])

            def f_logits():
                pe.wait_ge(drained("f_xT"), k.done("f_xT"))
                three(bank_of("f_l")[0:E, :], (gwh[:, :], gwl[:, :]), (fxh[:, :], fxl[:, :])).then_inc(filled("f_l"), 1)

            def f_lT():
                pe.wait_ge(drained("f_l"), k.done("f_l"))
                for c in range(CH):
                    ins = mm(bank_of("f_lT")[:, c * E:(c + 1) * E], gT[:, cs(c)], ident[0:E, 0:E], start=True, stop=True)
                ins.then_inc(filled("f_lT"), 1)

            def f_gT():
                pe.wait_ge(S("f_gate"), k.at("f_gate", 1))
                transposes("f_gT", lambda c: gate[:, c, :], E)

            def f_tile(i):
                if i < NT:
                    use = f"f_z{i}"
                    pe.wait_ge(drained(use), k.before(use))
                    three(bank_of(use)[:, :], (w1h[:, i, :], w1l[:, i, :]), (fxh[:, :], fxl[:, :])).then_inc(filled(use), 1)
                e = gates_at(i)
                if e is not None:
                    use, one = f"f_gb{e}", identr[0:E, e:e + 1].broadcast_to([E, P])
                    if i == 0:
                        pe.wait_ge(drained("f_gT"), k.done("f_gT"))
                    else:
                        pe.wait_ge(drained(use), k.before(use))
                    mm(bank_of(use)[:, :], one, gTh[:, :], start=True, stop=False)
                    mm(bank_of(use)[:, :], one, gTl[:, :], start=False, stop=True).then_inc(filled(use), 1)
                n = i - OUT_LAG
                if n >= 0:
                    pe.wait_ge(S("f_hi"), k.at("f_hi", n + 1))
                    lo, nth = lo_of(n)
                    pe.wait_ge(S(lo), k.at(lo, nth))
                    if n == 0:
                        pe.wait_ge(drained("f_o"), k.before("f_o"))
                    three(bank_of("f_o")[:, :], (w2h[:, n, :], w2l[:, n, :]), (hh[:, n % HBUF, :], hl[:, n % HBUF, :]),
                          start=(n == 0), stop=False).then_inc(k.gives("f_h_used"), 1)

            def f_out(x, last):
                mm(bank_of("f_o")[:, :], cb[:, :], gT, start=False, stop=True).then_inc(filled("f_o"), 1)

            def f_outT(x, last):
                pe.wait_ge(drained("f_o"), k.done("f_o"))
                transposes("f_oT", lambda c: oT[:, cs(c)])

            def n_xT():
                pe.wait_ge(S("n_xhat"), k.at("n_xhat", 1))
                transposes("n_xT", lambda c: xhat[:, c, :])

            def b_qk(g):
                if g == 0:
                    pe.wait_ge(drained("n_xT"), k.normed())
                for i, use in enumerate((f"b_q{g}", f"b_k{g}")):
                    w = i * GB + g
                    pe.wait_ge(drained(use), k.before(use))
                    three(bank_of(use)[:, :], (wqkh[:, w, :], wqkl[:, w, :]), (bxh[:, :], bxl[:, :])).then_inc(filled(use), 1)

            def b_v(n):
                use, w = f"b_v{n}", slice(n % 2 * 512, n % 2 * 512 + 512)
                pe.wait_ge(drained(use), k.before(use))
                three(bank_of(use)[:, :], (bxh[:, cs(n // 2)], bxl[:, cs(n // 2)]), (wbvh[:, w], wbvl[:, w])).then_inc(filled(use), 1)

            def b_vp(n):
                if n == 0:
                    pe.wait_ge(S("b_xprel"), k.at("b_xprel", 1))
                    pe.wait_ge(drained("b_vpre"), k.before("b_vpre"))
                for p in (2 * n, 2 * n + 1):
                    ins = three(bank_of("b_vpre")[:, p * CH:(p + 1) * CH], (wbvh[:, cs(p)], wbvl[:, cs(p)]), (xpreh[:, :], xprel[:, :]))
                if n == NPAIR // 2 - 1:
                    ins.then_inc(filled("b_vpre"), 1)

            def b_s(h):
                g, r = h // 4, slice(h % 4 * 32, h % 4 * 32 + 32)
                if h % 4 == 0:
                    for use in (f"b_q{g}", f"b_k{g}"):
                        if drained(use) is not drained(f"b_s{h}_0"):
                            pe.wait_ge(drained(use), k.done(use))
                for j in range(CH):
                    use = f"b_s{h}_{min(j, 2)}"
                    if j < 3:
                        pe.wait_ge(drained(use), k.before(use))
                    at = 2 * P if j == 3 else 0
                    o, w = bank_of(use)[:, at:at + T - j * P], kk[r, g % 2, cs(j)]
                    mm(o, w, q1[r, g % 2, j * P:T], start=True, stop=False)
                    ins = mm(o, w, q2[r, g % 2, j * P:T], start=False, stop=True)
                    if j != 2:
                        ins.then_inc(filled(use), 1)

            def b_av(p):
                if p == 0:
                    for n in range(2 * CH - 3, 2 * CH):
                        pe.wait_ge(drained(f"b_v{n}"), k.done(f"b_v{n}"))
                use = f"b_y{p}"
                pe.wait_ge(S("b_diag"), k.at("b_diag", 2 * p + 2))
                pe.wait_ge(drained(use), k.before(use))
                for j in range(CH):
                    for u in range(2):
                        h = 2 * p + u
                        ins = mm(bank_of(use)[DB * u:DB * u + DB, j * P:T], vv[:, j, h * DB:(h + 1) * DB],
                                 pflat[h % PBUF][:, j * (T + P):(j + 1) * T], start=(j == 0), stop=(j == CH - 1))
                ins.then_inc(filled(use), 1)

            def b_ss(p):
                pe.wait_ge(S("b_ysq"), k.at("b_ysq", p + 1))
                pe.wait_ge(drained(f"b_ss{p}"), k.before(f"b_ss{p}"))
                for c in range(CH):
                    ins = mm(bank_of(f"b_ss{p}")[:, 2 * c:2 * c + 2], ysq[p % 2][:, cs(c)], pairsel[:, :], start=True, stop=True)
                ins.then_inc(filled(f"b_ss{p}"), 1)

            def b_rT(i):
                n = pairs_of(i)
                pe.wait_ge(S("b_rr"), k.at("b_rr", EARLY if i == 0 else NPAIR))
                transposes(f"b_rT{i}", lambda c: rr[:, c, i * EARLY:i * EARLY + n, :].rearrange("p q a -> p (q a)"), 2 * n)

            def b_rb(p):
                use, i = f"b_rb{p}", p // EARLY
                n = 2 * pairs_of(i)
                if p % EARLY == 0:
                    pe.wait_ge(drained(f"b_rT{i}"), k.done(f"b_rT{i}"))
                pe.wait_ge(drained(use), k.before(use))
                mm(bank_of(use)[:, :], hsel[0:n, p % EARLY, :], rTh[0:n, :], start=True, stop=False)
                mm(bank_of(use)[:, :], hsel[0:n, p % EARLY, :], rTl[0:n, :], start=False, stop=True).then_inc(filled(use), 1)

            def b_wo(p):
                pe.wait_ge(drained(f"b_rb{p}"), k.done(f"b_rb{p}"))
                if p == 0:
                    pe.wait_ge(drained("b_o"), k.before("b_o"))
                ins = mm(bank_of("b_o")[:, :], wbo[:, p, :], ysb[:, p, :], start=(p == 0), stop=(p == NPAIR - 1))
                if p == NPAIR - 1:
                    ins.then_inc(filled("b_o"), 1)

            def b_outT(x, last):
                pe.wait_ge(drained("b_o"), k.done("b_o"))
                transposes("b_outT", lambda c: boT[:, cs(c)])

            run(k, pe, {"s_c": s_c, "s_cT": s_cT, "s_end": s_end, "m_xT": m_xT, "n_xT": n_xT, "a_proj": a_proj, "a_scale": a_scale, "a_qkT": a_qkT, "a_lags": a_lags, "a_den": a_den, "a_kends": a_kends,
                        "a_level": a_level, "a_state": a_state, "a_y": a_y, "a_out": a_out,
                        "f_xT": f_xT, "f_logits": f_logits, "f_lT": f_lT, "f_gT": f_gT, "f_tile": f_tile, "f_out": f_out, "f_outT": f_outT,
                        "b_qk": b_qk, "b_v": b_v, "b_vp": b_vp, "b_s": b_s, "b_av": b_av, "b_ss": b_ss, "b_rT": b_rT,
                        "b_rb": b_rb, "b_wo": b_wo, "b_outT": b_outT})

        @block.vector
        def _(dve):
            k = Count()
            tt, ts, stt, copy = dve.tensor_tensor, dve.tensor_scalar, dve.scalar_tensor_tensor, dve.tensor_copy
            setup = [0]

            def settled(ins):
                setup[0] += 1
                ins.then_inc(S("dve_setup"), 1)
                dve.wait_ge(S("dve_setup"), setup[0])

            dve.memset(headsum[:, :], 0.0)
            settled(dve.memset(pairsel[:, :], 0.0))
            for h in range(HA):
                r = slice(32 * h, 32 * h + 32)
                dve.memset(headsum[r, r], 1.0)
            dve.memset(pairsel[0:64, 0:1], 1.0)
            dve.memset(pairsel[64:P, 1:2], 1.0)
            dve.memset(whead[:, :, :], 0.0)
            dve.memset(xTs[:, 0:1], 0.0)
            dve.memset(xpre[:, 0:1], 0.0)
            for t in (eq, eq2, eq4):
                dve.memset(t[:, :, 0:E], 0.0)
            for i in range(FREE_AT_1, 8):
                dve.memset(unread[:, i:i + 1], 0.0).then_inc(S(f"drained{i}"), 1)
                dve.memset(unread[:, 8 + i:9 + i], 0.0).then_inc(S(f"filled{i}"), 1)
            dve.memset(unread[:, 0:1], 0.0).then_inc(S("xout_free"), 1)
            dve.memset(wpow[:, 0:1], 1.0)
            settled(dve.memset(wrev[:, P:P + 1], 1.0))
            dve.wait_ge(S("ident"), 1)
            copy(identr[:, :], ident[:, :])
            copy(hsel[:, :, :].rearrange("h q (u n) -> h (q u) n", u=2), ident[0:2 * EARLY, 0:2 * EARLY].unsqueeze(2).broadcast_to([2 * EARLY, 2 * EARLY, DB]))
            settled(dve.tensor_reduce(half[:, :], ident[:, :].rearrange("p (a u f) -> p a u f", u=2, f=FB)[:, :, 1, :],
                                      mybir.AxisListType.XY, ALU.add))
            ts(sgn[:, :], half[:, :], 2.0, -1.0, ALU.mult, ALU.add)

            def s_pow():
                dve.wait_ge(S("causal"), 1)
                dve.wait_ge(S("pool_setup"), 2 * len(LEVELS) + 2)
                copy(lmask[:, :, :], lmask_f)
                dve.wait_ge(S("w"), 1)
                copy(wpow[:, 1:2], decay[:, 1:2])
                settled(copy(wrev[:, P - 1:P], decay[:, 1:2]))
                n = 1
                while n < P:
                    w = wpow[:, n:n + 1]
                    ts(wpow[:, n + 1:2 * n + 1], wpow[:, 1:n + 1], w, None, ALU.mult)
                    settled(ts(wrev[:, P - 2 * n:P - n], wrev[:, P - n:P], w, None, ALU.mult))
                    n *= 2
                for h in range(HA):
                    r = slice(32 * h, 32 * h + 32)
                    ins = copy(whead[r, h, :], wpow[r, 0:64])
                settled(ins)

            def s_lo(i):
                if i == 0:
                    dve.wait_ge(S("w_hi"), 1)
                    tt(w1l[:, :, :], w1in, f32(w1h[:, :, :]), ALU.subtract).then_inc(S("w1_split"), 1)
                elif i == 1:
                    dve.wait_ge(S("w_hi"), 2)
                    tt(wbvl[:, :], wbvin, f32(wbvh[:, :]), ALU.subtract)
                    ts(nb1[:, :], b1c, -1.0, None, ALU.mult)
                    dve.wait_ge(S("wb_in"), WB_IN)
                    ts(wbo[:, :, :], wbo[:, :, :], gcol, None, ALU.mult)
                elif i == 2:
                    dve.wait_ge(S("w_hi"), 5)
                    tt(gwl[:, :], gw[:, :], f32(gwh[:, :]), ALU.subtract)
                    hi = wqkh[:, :, :].rearrange("p g (h u f) -> p (g h) u f", u=2, f=FB)
                    lo = wqkl[:, :, :].rearrange("p g (h u f) -> p (g h) u f", u=2, f=FB)
                    src = wqkin.rearrange("p a (h f) -> p (a h) f", f=FB)
                    for u in range(2):
                        tt(lo[:, :, u, :], src, f32(hi[:, :, u, :]), ALU.subtract)
                else:
                    dve.wait_ge(S("w_hi"), 6)
                    tt(w2l[:, :, :], w2in, f32(w2h[:, :, :]), ALU.subtract)
                    dve.wait_ge(S("cb_full"), 1)
                    tt(cb[:, :], bank[5][0:E, 0:C], b2r[:, :], ALU.add).then_inc(S("setup_done"), 1)

            def stats(ph):
                def step(x, last):
                    if ph == "m":
                        dve.wait_ge(S(f"x_in{int(x is xs[1])}"), 16 if k.it is None else k.value(16, 32))
                    elif ph == "n":
                        dve.wait_ge(drained("f_oT"), k.before("n_xT"))
                    else:
                        use = "b_outT" if last else "a_o"
                        dve.wait_ge(drained(use), k.before_slot(use))
                    for c in range(CH):
                        ins = dve.bn_stats(st6[:, c, :], x[:, c, :])
                    ins.then_inc(k.gives(f"step_{ph}_dve"), 1)
                    dve.wait_ge(S(f"step_{ph}_dve"), k.now(f"step_{ph}_dve"))
                    dve.memset(tick[:, :], 0.0)
                    for c in range(CH):
                        ins = dve.bn_aggr(mv[:, c, :], st6[:, c, :])
                    ins.then_inc(k.gives(f"{ph}_mv"), 1)
                return step

            def norm_x(ph):
                def step(x, last):
                    dve.wait_ge(S(f"{ph}_rstd"), k.at(f"{ph}_rstd", 1))
                    dve.wait_ge(drained(f"{ph}_xT"), k.before(f"{ph}_xT"))
                    for c in range(CH):
                        ins = ts(xhat[:, c, :], x[:, c, :], mv[:, c, 0:1], rstd[:, c:c + 1], ALU.subtract, ALU.mult)
                    ins.then_inc(k.gives(f"{ph}_xhat"), 1)
                return step

            def a_mix():
                dve.wait_ge(drained("m_xT"), k.normed())
                tt(xdiff, xTs[:, 1:T + 1], xTs[:, 0:T], ALU.subtract).then_inc(k.gives("step_a_dve"), 1)
                dve.wait_ge(S("step_a_dve"), k.now("step_a_dve"))
                for n in "qkvg":
                    stt(xm[n], xdiff, mix[n], xTs[:, 0:T], ALU.mult, ALU.add).then_inc(k.gives("a_xm"), 1)

            def a_scale():
                dve.wait_ge(S("a_nrm"), k.at("a_nrm", 1))
                ts(nrme[:, :], nrm[:, :], Q_EPS, None, ALU.add).then_inc(k.gives("step_a_dve"), 1)
                dve.wait_ge(S("step_a_dve"), k.now("step_a_dve"))
                dve.reciprocal(rn[:, :], nrme[:, :]).then_inc(k.gives("step_a_dve"), 1)
                dve.wait_ge(S("step_a_dve"), k.now("step_a_dve"))
                for i, n in enumerate("qk"):
                    for c in range(CH):
                        ins = ts(qk_n[:, i, c, :], bank_of(f"a_{n}")[:, cs(c)], rn[:, i * CH + c:i * CH + c + 1], None, ALU.mult)
                    ins.then_inc(drained(f"a_{n}"), 1)

            def a_products():
                dve.wait_ge(drained("a_qT"), k.done("a_qT"))
                dve.wait_ge(drained("a_kT"), k.done("a_kT"))
                for lag in range(LAGS):
                    n = LAGS - lag
                    stt(lag_part(lagp, lag), lag_view(ke, 0, n), wpow[:, lag:lag + 1], lag_view(qe, lag, n), ALU.mult, ALU.mult)\
                        .then_inc(k.gives("a_lagp"), 1)

            def a_z():
                dve.tensor_tensor_scan(z, wpow[:, 1:2].broadcast_to([P, T]), ke, 0.0, ALU.mult, ALU.add).then_inc(k.gives("step_a_dve"), 1)
                dve.wait_ge(S("step_a_dve"), k.now("step_a_dve"))
                tt(qz, qe, z, ALU.mult).then_inc(k.gives("a_qz"), 1)

            def q_level(i):
                tt(*q_times_w(i), ALU.mult).then_inc(k.gives("a_qlev"), 1)

            def a_lags():
                dve.wait_ge(drained("a_vT"), k.done("a_vT"))
                dve.wait_ge(filled("a_r0"), k.done("a_r0"))
                tt(ylag, bank_of("a_r0")[:, :], vch, ALU.mult).then_inc(drained("a_r0"), 1)
                for lag, at, use in ((1, 0, "a_r1"), (2, 0, "a_r23"), (3, 256, "a_r23")):
                    if lag < 3:
                        dve.wait_ge(filled(use), k.done(use))
                    n = LAGS - lag
                    ins = tt(lag_part(ytmp, lag, T), bank_of(use)[:, at:at + n * P].rearrange("p (b l) -> p b l", l=n), lag_view(vch, 0, n), ALU.mult)
                    if lag != 2:
                        ins.then_inc(drained(use), 1)

            def a_rden():
                dve.wait_ge(filled("a_den"), k.done("a_den"))
                dve.reciprocal(rden, bank_of("a_den")[:, :]).then_inc(drained("a_den"), 1)

            def a_level(i):
                if i == 0:
                    dve.wait_ge(S("a_pmat"), k.at("a_pmat", 1))
                else:
                    dve.wait_ge(drained(f"a_s{i - 1}_1"), k.done(f"a_s{i - 1}_1"))
                n = 2 ** LEVELS[i]
                m = lmask[:, i, :].rearrange("p (b n) -> p b n", n=n).unsqueeze(2).broadcast_to([P, 64 // n, HA, n])
                for u in range(2):
                    use = f"a_s{i}_{u}"
                    dve.wait_ge(filled(use), k.done(use))
                    dve.memset(unread[:, i % 2 * 2 + u:i % 2 * 2 + u + 1], 0.0)
                    for c in range(2):
                        o = pmat[:, :, 2 * u + c, :].rearrange("p h (b u n) -> p b u h n", u=2, n=n)[:, :, 1, :, :]
                        d = bank_of(use)[:, c * 256:(c + 1) * 256].rearrange("p (b h n) -> p b h n", h=HA, n=n)
                        ins = dve.copy_predicated(o, m, d)
                    ins.then_inc(drained(use), 1)

            def a_state():
                dve.wait_ge(filled("a_u"), k.done("a_u"))
                m = headsum[:, :].unsqueeze(1).broadcast_to([P, CH - 1, P])
                tt(states[:, :, :], bank_of("a_u")[:, 0:3 * P].rearrange("p (c n) -> p c n", c=3), m, ALU.mult).then_inc(drained("a_u"), 1)
                dve.wait_ge(drained("a_u"), k.done("a_u"))
                for c in (1, 2):
                    stt(states[:, c, :], states[:, c - 1, :], wpow[:, P:P + 1], states[:, c, :], ALU.mult, ALU.add)\
                        .then_inc(k.gives("a_states"), 1)
                    if c == 1:
                        dve.wait_ge(S("a_states"), k.now("a_states"))

            def a_att():
                dve.wait_ge(drained("a_g"), k.done("a_g"))
                stt(gr, gth, 1.0, rden, ALU.add, ALU.mult)
                dve.wait_ge(S("a_ylag"), k.at("a_ylag", LAGS - 1))
                dve.wait_ge(filled("a_y"), k.done("a_y"))
                tt(ysum, bank_of("a_y")[:, :], ylag, ALU.add).then_inc(drained("a_y"), 1)
                dve.wait_ge(drained("a_y"), k.done("a_y"))
                stt(att, ysum, 0.5, gr, ALU.mult, ALU.mult).then_inc(k.gives("a_att"), 1)

            def a_out(x, last):
                dve.wait_ge(filled("a_o"), k.done("a_o"))
                tt(x[:, :, :], x[:, :, :], chunks(bank_of("a_o")[:, :]), ALU.add).then_inc(drained("a_o"), 1)

            def over_experts(v):
                return v.unsqueeze(2).broadcast_to([P, CH, E])

            def f_xT():
                dve.wait_ge(S("f_xh"), k.at("f_xh", 1))
                tt(fxl[:, :], bank_of("f_xT")[:, :], f32(fxh[:, :]), ALU.subtract).then_inc(drained("f_xT"), 1)

            def f_lT():
                dve.wait_ge(filled("f_lT"), k.done("f_lT"))
                bias = gbias[:, :].unsqueeze(1).broadcast_to([P, CH, E])
                tt(lg[:, :, :], bank_of("f_lT")[:, 0:CH * E].rearrange("p (c e) -> p c e", c=CH), bias, ALU.add).then_inc(drained("f_lT"), 1)
                dve.wait_ge(drained("f_lT"), k.done("f_lT"))
                dve.tensor_reduce(m1[:, :], lg[:, :, :], AX_X, ALU.max).then_inc(k.gives("step_f_dve"), 1)
                dve.wait_ge(S("step_f_dve"), k.now("step_f_dve"))
                tt(lg2[:, :, :], lg[:, :, :], over_experts(m1[:, :]), ALU.subtract).then_inc(k.gives("f_lg2"), 1)

            def f_choose():
                dve.wait_ge(S("f_ex"), k.at("f_ex", 1))
                dve.tensor_reduce(sm[:, :], ex[:, :, :], AX_X, ALU.add).then_inc(k.gives("step_f_dve"), 1)
                dve.wait_ge(S("step_f_dve"), k.now("step_f_dve"))
                dve.reciprocal(rs1[:, :], sm[:, :]).then_inc(k.gives("step_f_dve"), 1)
                dve.wait_ge(S("step_f_dve"), k.now("step_f_dve"))
                tt(pr[:, :, :], ex[:, :, :], over_experts(rs1[:, :]), ALU.mult).then_inc(k.gives("step_f_dve"), 1)
                dve.wait_ge(S("step_f_dve"), k.now("step_f_dve"))
                dve.memset(tick[:, :], 0.0)
                for c in range(CH):
                    ins = dve.max(top8[:, c, :], pr[:, c, :])
                ins.then_inc(k.gives("step_f_dve"), 1)
                dve.wait_ge(S("step_f_dve"), k.now("step_f_dve"))
                second = over_experts(top8[:, :, 1])
                tt(gt[:, :, :], pr[:, :, :], second, ALU.is_gt)
                tt(need[:, :], top8[:, :, 0], top8[:, :, 1], ALU.is_equal)
                tt(eq[:, :, E:], pr[:, :, :], second, ALU.is_equal).then_inc(k.gives("step_f_dve"), 1)
                dve.wait_ge(S("step_f_dve"), k.now("step_f_dve"))
                tt(eq2[:, :, E:], eq[:, :, E:], eq[:, :, E - 1:-1], ALU.add).then_inc(k.gives("step_f_dve"), 1)
                dve.wait_ge(S("step_f_dve"), k.now("step_f_dve"))
                tt(eq4[:, :, E:], eq2[:, :, E:], eq2[:, :, E - 2:-2], ALU.add).then_inc(k.gives("step_f_dve"), 1)
                dve.wait_ge(S("step_f_dve"), k.now("step_f_dve"))
                tt(eq8[:, :, :], eq4[:, :, E:], eq4[:, :, E - 4:-4], ALU.add).then_inc(k.gives("step_f_dve"), 1)
                dve.wait_ge(S("step_f_dve"), k.now("step_f_dve"))
                stt(keep[:, :, :], eq8[:, :, :], 1.0, over_experts(need[:, :]), ALU.subtract, ALU.is_le).then_inc(k.gives("step_f_dve"), 1)
                dve.wait_ge(S("step_f_dve"), k.now("step_f_dve"))
                tt(kept[:, :, :], keep[:, :, :], eq[:, :, E:], ALU.mult).then_inc(k.gives("step_f_dve"), 1)
                dve.wait_ge(S("step_f_dve"), k.now("step_f_dve"))
                tt(both[:, :, :], kept[:, :, :], gt[:, :, :], ALU.add).then_inc(k.gives("step_f_dve"), 1)
                dve.wait_ge(S("step_f_dve"), k.now("step_f_dve"))
                tt(gate[:, :, :], both[:, :, :], pr[:, :, :], ALU.mult).then_inc(k.gives("f_gate"), 1)

            def f_gT():
                dve.wait_ge(S("f_gTh"), k.at("f_gTh", 1))
                tt(gTl[:, :], bank_of("f_gT")[0:E, :], f32(gTh[:, :]), ALU.subtract).then_inc(drained("f_gT"), 1)

            def f_tile(i):
                if i < NT:
                    dve.wait_ge(drained(f"f_gb{i // 2}"), k.done(f"f_gb{i // 2}"))
                    dve.wait_ge(filled(f"f_z{i}"), k.done(f"f_z{i}"))
                    if i >= HBUF:
                        lo, nth = lo_of(i - HBUF)
                        dve.wait_ge(S(lo), k.at(lo, nth))
                    stt(hg[i % HBUF], bank_of(f"f_z{i}")[:, :], nb1[:, i:i + 1], gb[i // 2 % 2], ALU.max, ALU.mult)\
                        .then_inc(drained(f"f_z{i}"), 1)
                n = i - 1
                if 0 <= n < NT and n % LO_DVE == 0:
                    dve.wait_ge(S("f_hi"), k.at("f_hi", n + 1))
                    if n >= HBUF:
                        dve.wait_ge(S("f_h_used"), k.at("f_h_used", n - HBUF + 1))
                    tt(hl[:, n % HBUF, :], hg[n % HBUF], f32(hh[:, n % HBUF, :]), ALU.subtract).then_inc(k.gives("f_lo_dve"), 1)

            def f_outT(x, last):
                dve.wait_ge(filled("f_oT"), k.done("f_oT"))
                if last:
                    m, n = k.runs["f"]
                    dve.wait_ge(S("xout_free"), k.value(32, 16 * (n - 2) + 1))
                tt((xout if last else x)[:, :, :], x[:, :, :], chunks(bank_of("f_oT")[:, :]), ALU.add).then_inc(drained("f_oT"), 1)

            def n_xT():
                dve.wait_ge(S("n_xh"), k.at("n_xh", 1))
                tt(bxl[:, :], bank_of("n_xT")[:, :], f32(bxh[:, :]), ALU.subtract)
                dve.tensor_reduce(xsum[:, :], chunks(bank_of("n_xT")[:, :]), AX_X, ALU.add).then_inc(drained("n_xT"), 1)

            def b_qk(g):
                if g == 0:
                    dve.wait_ge(drained("n_xT"), k.normed())
                    copy(xpre[:, 1:2], xsum[:, 0:1]).then_inc(k.gives("step_b_dve"), 1)
                    dve.wait_ge(S("step_b_dve"), k.now("step_b_dve"))
                    tt(xpre[:, 2:3], xpre[:, 1:2], xsum[:, 1:2], ALU.add).then_inc(k.gives("step_b_dve"), 1)
                    dve.wait_ge(S("step_b_dve"), k.now("step_b_dve"))
                    tt(xpre[:, 3:4], xpre[:, 2:3], xsum[:, 2:3], ALU.add).then_inc(k.gives("b_xpre"), 1)
                dve.wait_ge(S("b_qk_hi"), k.at("b_qk_hi", 2 * g + 1))
                tt(q2[:, g % 2, :], bank_of(f"b_q{g}")[:, :], f32(q1[:, g % 2, :]), ALU.subtract).then_inc(drained(f"b_q{g}"), 1)
                dve.wait_ge(S("b_qk_hi"), k.at("b_qk_hi", 2 * g + 2))
                stt(kk[:, g % 2, :], bank_of(f"b_k{g}")[:, :], half[:, :], f32(ksg[:, :]), ALU.mult, ALU.subtract).then_inc(drained(f"b_k{g}"), 1)

            def b_v(n):
                if n % 2:
                    dve.wait_ge(filled(f"b_v{n}"), k.done(f"b_v{n}"))
                    copy(vv[:, n // 2, 512:1024], bank_of(f"b_v{n}")[:, :]).then_inc(drained(f"b_v{n}"), 1)

            def b_xl():
                dve.wait_ge(S("b_xpreh"), k.at("b_xpreh", 1))
                tt(xprel[:, :], xpre[:, :], f32(xpreh[:, :]), ALU.subtract).then_inc(k.gives("b_xprel"), 1)

            def b_s(h):
                for j in (0, 1, 2):
                    dve.wait_ge(drained(f"b_s{h}_{j}"), k.done(f"b_s{h}_{j}"))
                d = pflat[h % PBUF][:, 0:CH * (T + P)].rearrange("p (j n) -> p j n", n=T + P)[:, :, 0:P]
                m = causal[:, :].unsqueeze(1).broadcast_to([P, CH, P])
                stt(d, d, 1.0, m, ALU.add, ALU.mult).then_inc(k.gives("b_diag"), 1)

            def b_y(p):
                dve.wait_ge(drained("b_vpre"), k.done("b_vpre"))
                dve.wait_ge(filled(f"b_y{p}"), k.done(f"b_y{p}"))
                v = vpre[:, p, :].unsqueeze(2).broadcast_to([P, CH, P])
                tt(chunks(ysb[:, p, :]), chunks(bank_of(f"b_y{p}")[:, :]), v, ALU.add).then_inc(drained(f"b_y{p}"), 1)

            def b_ss(p):
                dve.wait_ge(filled(f"b_ss{p}"), k.done(f"b_ss{p}"))
                ts(ssv[:, p, :, :].rearrange("p c a -> p (c a)"), bank_of(f"b_ss{p}")[:, 0:2 * CH], 1.0 / DB, 4 * RMS_EPS, ALU.mult, ALU.add)\
                    .then_inc(drained(f"b_ss{p}"), 1)

            def b_rT(i):
                n = 2 * pairs_of(i)
                dve.wait_ge(S("b_rTh"), k.at("b_rTh", i + 1))
                tt(rTl[0:n, :], bank_of(f"b_rT{i}")[0:n, :], f32(rTh[0:n, :]), ALU.subtract).then_inc(drained(f"b_rT{i}"), 1)

            def b_rb(p):
                dve.wait_ge(filled(f"b_rb{p}"), k.done(f"b_rb{p}"))
                tt(ysb[:, p, :], ysb[:, p, :], bank_of(f"b_rb{p}")[:, :], ALU.mult).then_inc(drained(f"b_rb{p}"), 1)

            def b_outT(x, last):
                dve.wait_ge(filled("b_outT"), k.done("b_outT"))
                tt(x[:, :, :], x[:, :, :], chunks(bank_of("b_outT")[:, :]), ALU.add).then_inc(drained("b_outT"), 1)

            run(k, dve, {"m_stats": stats("m"), "n_stats": stats("n"), "f_stats": stats("f"), "m_xhat": norm_x("m"), "n_xhat": norm_x("n"),
                         "f_xhat": norm_x("f"), "s_pow": s_pow, "s_lo": s_lo, "n_xT": n_xT, "a_mix": a_mix, "a_scale": a_scale, "a_products": a_products, "a_z": a_z, "a_q": q_level, "a_lags": a_lags,
                         "a_rden": a_rden, "a_level": a_level, "a_state": a_state, "a_att": a_att, "a_out": a_out,
                         "f_xT": f_xT, "f_lT": f_lT, "f_choose": f_choose, "f_gT": f_gT, "f_tile": f_tile, "f_outT": f_outT,
                         "b_qk": b_qk, "b_v": b_v, "b_xl": b_xl, "b_s": b_s, "b_y": b_y, "b_ss": b_ss, "b_rT": b_rT,
                         "b_rb": b_rb, "b_outT": b_outT})




def _laid_out(inputs):
    import numpy as np

    i = {n: np.asarray(v) for n, v in inputs.items()}
    a = {"x": i["L0_attn_a_x"], "WaT": np.stack([i[f"L0_attn_a_W{n}"].T for n in "qkvgo"], axis=1)}
    g, b1 = i["L0_attn_b_g_weight"], i["L0_ffn_b1"].reshape(NT, P)
    a["cols"] = np.stack([i[f"L0_attn_a_mix_{n}"].reshape(P) for n in "qkvg"] + [i["L0_attn_a_norm_scale"], i["L0_attn_a_time_decay"],
                         np.concatenate([g, g])] + list(b1), axis=1)
    a["WbqkT"] = np.stack([i["L0_attn_b_Wq"].T, i["L0_attn_b_Wk"].T], axis=1)
    a["WbvT"] = i["L0_attn_b_Wv"].T
    a["WboT"] = i["L0_attn_b_Wo"].T.reshape(NPAIR, P, C).transpose(1, 0, 2)
    a["gate_wT"], a["gate_b"] = i["L0_ffn_gate_w"].T, i["L0_ffn_gate_b"]
    a["w1L"] = i["L0_ffn_w1"].transpose(1, 0, 2).reshape(C, NT, P)
    a["w2L"] = i["L0_ffn_w2"].reshape(NT, P, C).transpose(1, 0, 2)
    a["b2"] = i["L0_ffn_b2"]
    return {n: np.ascontiguousarray(v) for n, v in a.items()}


def kernel(**inputs):
    import concourse.bacc as _bacc
    from concourse.bass_utils import run_bass_kernel_spmd as _run

    arrays = _laid_out(inputs)
    nc = _bacc.Bacc("TRN2", target_bir_lowering=False, num_devices=1)
    args = {n: nc.dram_tensor(f"in_{n}", v.shape, mybir.dt.from_np(v.dtype), kind="ExternalInput").ap() for n, v in arrays.items()}
    out = nc.dram_tensor("result", (B, T, C), F32, kind="ExternalOutput").ap()
    hybrid_block_kernel(nc, args, out)
    return _run(nc, [{f"in_{n}": v for n, v in arrays.items()}], core_ids=[0]).results[0]["result"]
```
